# Optimizing a Trainium2 kernel written in Bass

```python
import numpy as np
import jax
import jax.numpy as jnp

def _softmax(x, axis=-1):
    return jax.nn.softmax(x, axis=axis)

def _gelu(x):
    return jax.nn.gelu(x, approximate=True)

def _silu(x):
    return jax.nn.silu(x)

def _sigmoid(x):
    return jax.nn.sigmoid(x)

def _layernorm(x, axis=-1, eps=1e-05):
    m = jnp.mean(x, axis=axis, keepdims=True)
    v = jnp.var(x, axis=axis, keepdims=True)
    return (x - m) / jnp.sqrt(v + eps)

def _scatter_add(tgt, idx, src, axis=0):
    return tgt.at[idx].add(src)

def _segment_sum(src, seg, n):
    return jax.ops.segment_sum(src, seg, n)
kernel_name = 'mk_gnn_ffn_d1_gnn_r32_19ca11'

def setup_inputs(seed: int=0):
    np.random.seed(seed)
    _w = jnp.asarray

    def _rec_inputs():
        import jax
        import jax.numpy as jnp
        _gk = jax.random.key(seed)
        x = -8.776e-05 + 1 * jax.random.normal(jax.random.fold_in(_gk, 1), (625, 256), jnp.float32)
        src = jax.random.randint(jax.random.fold_in(_gk, 2), (10000,), 0, 625, jnp.int32)
        dst = jax.random.randint(jax.random.fold_in(_gk, 3), (10000,), 0, 625, jnp.int32)
        _o = jnp.argsort(dst, stable=True)
        src = src[_o]
        dst = dst[_o]
        edge_weight = jax.random.uniform(jax.random.fold_in(_gk, 12), (10000,), jnp.float32, 0.0, 0.999998)
        return (x, src, dst, edge_weight)
    x, src, dst, edge_weight = _rec_inputs()

    def _L0_gnn_setup():
        import jax, jax.numpy as jnp
        import numpy as np
        N = 625
        E = 10000
        D_IN = 256
        D_OUT = 256
        BN_EPS = 1e-05

        def _batchnorm(h, gamma, beta):
            mean = jnp.mean(h, axis=0)
            var = jnp.var(h, axis=0)
            return (h - mean) * jax.lax.rsqrt(var + BN_EPS) * gamma + beta
        key = jax.random.key(seed)
        ks = jax.random.split(key, 10)
        x = jax.random.normal(ks[0], (N, D_IN), dtype=jnp.float32)
        edge_index = jax.random.randint(ks[1], (2, E), 0, N, dtype=jnp.int64)
        edge_weight = jax.random.uniform(ks[2], (E,), dtype=jnp.float32)
        s1 = 1.0 / np.sqrt(D_IN)
        s2 = 1.0 / np.sqrt(D_OUT)
        W1 = jax.random.uniform(ks[3], (D_IN, D_OUT), minval=-s1, maxval=s1, dtype=jnp.float32)
        b1 = jax.random.uniform(ks[4], (D_OUT,), minval=-s1, maxval=s1, dtype=jnp.float32)
        g1 = jnp.ones((D_OUT,), jnp.float32)
        be1 = jnp.zeros((D_OUT,), jnp.float32)
        W2 = jax.random.uniform(ks[5], (D_OUT, D_OUT), minval=-s2, maxval=s2, dtype=jnp.float32)
        b2 = jax.random.uniform(ks[6], (D_OUT,), minval=-s2, maxval=s2, dtype=jnp.float32)
        g2 = jnp.ones((D_OUT,), jnp.float32)
        be2 = jnp.zeros((D_OUT,), jnp.float32)
        eps = jnp.zeros((1,), jnp.float32)
        return {'x': x, 'edge_index': edge_index, 'edge_weight': edge_weight, 'W1': W1, 'b1': b1, 'g1': g1, 'be1': be1, 'W2': W2, 'b2': b2, 'g2': g2, 'be2': be2, 'eps': eps}
    _L0_gnn_all = _L0_gnn_setup()
    _L0_gnn_in = {k: v for k, v in _L0_gnn_all.items() if k in ('W1', 'b1', 'g1', 'be1', 'W2', 'b2', 'g2', 'be2', 'eps')}
    del _L0_gnn_all

    def _L0_ffn_setup():
        import jax, jax.numpy as jnp
        import numpy as np
        D_IN, D_HID, D_OUT = (256, 512, 256)
        N_EXPERTS, TOP_K = (64, 2)
        B, S = (8, 128)
        key = jax.random.key(seed)
        ks = jax.random.split(key, 8)
        scale_in = 1.0 / np.sqrt(D_IN)
        scale_hid = 1.0 / np.sqrt(D_HID)
        return {'x': jax.random.normal(ks[0], (B, S, D_IN), dtype=jnp.float32), 'Wr': jax.random.uniform(ks[1], (D_IN, N_EXPERTS), jnp.float32, -scale_in, scale_in), 'br': jax.random.uniform(ks[2], (N_EXPERTS,), jnp.float32, -scale_in, scale_in), 'W1': jax.random.uniform(ks[3], (N_EXPERTS, D_IN, D_HID), jnp.float32, -scale_in, scale_in), 'b1': jax.random.uniform(ks[4], (N_EXPERTS, D_HID), jnp.float32, -scale_in, scale_in), 'W2': jax.random.uniform(ks[5], (N_EXPERTS, D_HID, D_OUT), jnp.float32, -scale_hid, scale_hid), 'b2': jax.random.uniform(ks[6], (N_EXPERTS, D_OUT), jnp.float32, -scale_hid, scale_hid)}
    _L0_ffn_all = _L0_ffn_setup()
    _L0_ffn_in = {k: v for k, v in _L0_ffn_all.items() if k in ('Wr', 'br', 'W1', 'b1', 'W2', 'b2')}
    del _L0_ffn_all
    return {'x': x, 'src': src, 'dst': dst, 'edge_weight': edge_weight, 'L0_gnn_W1': _L0_gnn_in['W1'], 'L0_gnn_b1': _L0_gnn_in['b1'], 'L0_gnn_g1': _L0_gnn_in['g1'], 'L0_gnn_be1': _L0_gnn_in['be1'], 'L0_gnn_W2': _L0_gnn_in['W2'], 'L0_gnn_b2': _L0_gnn_in['b2'], 'L0_gnn_g2': _L0_gnn_in['g2'], 'L0_gnn_be2': _L0_gnn_in['be2'], 'L0_gnn_eps': _L0_gnn_in['eps'], 'L0_ffn_Wr': _L0_ffn_in['Wr'], 'L0_ffn_br': _L0_ffn_in['br'], 'L0_ffn_W1': _L0_ffn_in['W1'], 'L0_ffn_b1': _L0_ffn_in['b1'], 'L0_ffn_W2': _L0_ffn_in['W2'], 'L0_ffn_b2': _L0_ffn_in['b2']}

def reference(x, src, dst, edge_weight, L0_gnn_W1, L0_gnn_b1, L0_gnn_g1, L0_gnn_be1, L0_gnn_W2, L0_gnn_b2, L0_gnn_g2, L0_gnn_be2, L0_gnn_eps, L0_ffn_Wr, L0_ffn_br, L0_ffn_W1, L0_ffn_b1, L0_ffn_W2, L0_ffn_b2):
    import jax
    import jax.numpy as jnp

    def _L0_gnn_ref(x, edge_index, edge_weight, W1, b1, g1, be1, W2, b2, g2, be2, eps):
        import jax, jax.numpy as jnp
        import numpy as np
        N = 625
        E = 10000
        D_IN = 256
        D_OUT = 256
        BN_EPS = 1e-05

        def _batchnorm(h, gamma, beta):
            mean = jnp.mean(h, axis=0)
            var = jnp.var(h, axis=0)
            return (h - mean) * jax.lax.rsqrt(var + BN_EPS) * gamma + beta
        src = edge_index[0]
        dst = edge_index[1]
        msg = edge_weight[:, None] * x[src]
        agg = jax.ops.segment_sum(msg, dst, num_segments=N)
        out = agg + (1.0 + eps[0]) * x
        h = out @ W1 + b1
        h = _batchnorm(h, g1, be1)
        h = h @ W2 + b2
        h = _batchnorm(h, g2, be2)
        return h

    def _L0_ffn_ref(x, Wr, br, W1, b1, W2, b2):
        import jax, jax.numpy as jnp
        import numpy as np
        D_IN, D_HID, D_OUT = (256, 512, 256)
        N_EXPERTS, TOP_K = (64, 2)
        B, S = (8, 128)
        Bx, Sx, D = x.shape
        xf = x.reshape(-1, D)
        T = xf.shape[0]
        E = Wr.shape[1]
        logits = xf @ Wr + br
        topk_logits, topk_idx = jax.lax.top_k(logits, TOP_K)
        gates = jax.nn.softmax(topk_logits, axis=1)
        combine = jnp.zeros((T, E), xf.dtype).at[jnp.arange(T)[:, None], topk_idx].add(gates)
        out = jnp.zeros((T, W2.shape[-1]), xf.dtype)
        for e in range(E):
            h = jax.nn.relu(xf @ W1[e] + b1[e])
            y = h @ W2[e] + b2[e]
            out = out + combine[:, e:e + 1] * y
        return out.reshape(Bx, Sx, -1)
    edge_index = jnp.stack([src, dst])
    x = x + _L0_gnn_ref(_layernorm(x, axis=-1), edge_index, edge_weight, L0_gnn_W1, L0_gnn_b1, L0_gnn_g1, L0_gnn_be1, L0_gnn_W2, L0_gnn_b2, L0_gnn_g2, L0_gnn_be2, L0_gnn_eps)
    x = x + _L0_ffn_ref(_layernorm(x, axis=-1)[None], L0_ffn_Wr, L0_ffn_br, L0_ffn_W1, L0_ffn_b1, L0_ffn_W2, L0_ffn_b2)[0]
    return x

_drawn_inputs = setup_inputs


def setup_inputs(seed=0):
    import zlib

    import numpy as np

    out = dict(_drawn_inputs(seed))
    spreads = {'L0_gnn_g1': (1.0, 0.2),
     'L0_gnn_be1': (0.0, 0.8),
     'L0_gnn_g2': (1.0, 0.2),
     'L0_gnn_be2': (0.0, 0.1)}
    factors = {'L0_gnn_b1': 8.0, 'L0_gnn_b2': 8.0, 'L0_ffn_b1': 7.78, 'L0_ffn_b2': 4.463}
    for name, (base, spread) in spreads.items():
        noise = np.random.default_rng([zlib.crc32(name.encode()), seed]).standard_normal(out[name].shape)
        drawn = base * np.exp(spread * noise) if base else spread * noise
        out[name] = jnp.asarray(drawn.astype(out[name].dtype))
    for name, factor in factors.items():
        out[name] = (out[name] * factor).astype(out[name].dtype)
    return out
```

```python
import concourse.bass as bass
from concourse import mybir
from contextlib import ExitStack

FP32 = mybir.dt.float32
BF16 = mybir.dt.bfloat16
FP16 = mybir.dt.float16
I32 = mybir.dt.int32
U32 = mybir.dt.uint32
ALU = mybir.AluOpType
ACT = mybir.ActivationFunctionType
AX = mybir.AxisListType

NODES, EDGES, D, HID, EXPERTS, TOPK = 625, 10000, 256, 512, 64, 2
NT, NP = 5, 125
GROUPS, QUADS, EP = 20, 4, 125
GE = QUADS * EP
WIN = 64
ROUNDS = -(-NODES // WIN)
AT_W = NODES - 1 + WIN
PARTS = 3
CAP = 64
PAIRS = EXPERTS // 2
MAX_OVER = (NODES * TOPK - 2) // CAP
OVER_PAIRS = (MAX_OVER + 1) // 2
ALL_PAIRS = PAIRS + OVER_PAIRS
RING = 8
XG = 4
EPS = 1e-5
C0 = 320
CHUNKS = [(0, C0), (C0, NODES)]
NVEC = 12


def gnn_moe(nc, x, src, dst, ew, W1, b1, g1, be1, W2, b2, g2, be2, eps, Wr, br, F1, fb1, F2, fb2, out):
    ctx = ExitStack()
    with ctx:
        def sb(name, shape, dt=FP32):
            return ctx.enter_context(nc.sbuf_tensor(name, shape, dt))

        def sem(name):
            return ctx.enter_context(nc.semaphore(name))

        def region(name, words, tensors):
            tile = sb(name, [128, words])

            def cut(*wanted):
                at, views = 0, []
                for shape, dt in wanted:
                    count = 1
                    for n in shape[1:]:
                        count *= n
                    size = -(-count * (2 if dt in (BF16, FP16) else 4) // 4)
                    assert at + size <= words, (name, at + size)
                    v = tile[0:shape[0], at:at + size]
                    if dt != FP32:
                        v = v.bitcast(dt)
                    letters = "abcd"[0:len(shape) - 1]
                    v = v.rearrange(f"p ({' '.join(letters)}) -> p {' '.join(letters)}",
                                    **dict(zip(letters, shape[1:])))
                    views.append(v)
                    at += size
                return views

            return [cut(*t) for t in tensors]

        xf_dram = nc.dram_tensor("xf_rows", [NODES, D], FP32).ap()
        y_dram = nc.dram_tensor("y_rows", [ALL_PAIRS * 128, D], FP32).ap()

        w1r = sb("w1_ring", [128, RING, 2, 2 * HID])
        w2r = sb("w2_ring", [128, RING, 2, 4 * D])
        ident = sb("ident", [128, 128])
        iota_src = sb("iota_src", [128, NT, 128], FP16)
        iota_c = sb("iota_c", [128, 128], FP16)
        tri = sb("tri", [NP, NP], BF16)
        ones_b = sb("ones_b", [NP, NP], BF16)
        ones_r = sb("ones_r", [1, NP])
        e64 = sb("e64", [NP, EXPERTS])
        tok = sb("tok", [NP, NT])
        w64 = sb("w64", [1, ROUNDS, GROUPS])
        bi = sb("bi", [1, 2 * OVER_PAIRS])
        pi2 = sb("pi2", [1, OVER_PAIRS])
        xs = sb("xs", [NP, NT, D])
        AWs = sb("AWs", [128, 2, NT, WIN])
        Dw = sb("Dw", [EP, 2, QUADS, PARTS, WIN], BF16)
        w1g = sb("w1g", [128, 2, D])
        w2g = sb("w2g", [128, 2, D])
        wrs = sb("wrs", [128, 2, EXPERTS])
        brs = sb("brs", [1, EXPERTS])
        vec = sb("vec", [NVEC, 128])
        vecT = sb("vecT", [128, NVEC])
        epsb = sb("epsb", [128, 1])
        dlo = sb("dlo", [GROUPS, 4])
        drow = sb("drow", [1, 2 * GROUPS])
        span = sb("span", [1, 1])
        flags = sb("flags", [1, ROUNDS], I32)
        bases_f = sb("bases_f", [1, ROUNDS, GROUPS])
        bases = sb("bases", [1, ROUNDS * GROUPS], I32)
        zero = sb("zero", [128, D])
        wb = sb("wb", [EP, GROUPS * QUADS], BF16)
        EF = sb("EF", [EP, GROUPS, 5 * QUADS])
        EFs = sb("EFs", [EP, 2 * 5 * QUADS])
        st = sb("st", [128, NT, 6])
        mv = sb("mv", [128, NT, 2])
        nrm = sb("nrm", [128, 6, NT])
        b1T = sb("b1T", [128, EXPERTS, 4])
        b2T = sb("b2T", [128, EXPERTS, 2])
        b1o = sb("b1o", [128, 2, 4])
        b2o = sb("b2o", [128, 2, 2])
        m8 = sb("m8", [NP, NT, 8])
        i8 = sb("i8", [NP, NT, 8], U32)
        ixf = sb("ixf", [NP, TOPK, NT])
        gt = sb("gt", [NP, 5, NT])
        Mb = sb("Mb", [NP, NT, EXPERTS], BF16)
        slf = sb("slf", [NP, TOPK * NT])
        sli = sb("sli", [NP, TOPK * NT], U32)
        lohi = sb("lohi", [NP, 2, TOPK * NT], U32)
        lhf = sb("lhf", [NP, 2, TOPK * NT])
        idx = sb("idx", [128, ALL_PAIRS], U32)
        idn = sb("idn", [128, RING], U32)
        oexp_f = sb("oexp_f", [1, 2 * OVER_PAIRS])
        oexp = sb("oexp", [1, 2 * OVER_PAIRS], I32)
        oflag = sb("oflag", [1, OVER_PAIRS], I32)
        (AT,), (xg, ys, hb) = region("adjacency", NT * AT_W, [
            [([128, NT, AT_W], FP32)],
            [([128, XG, D], FP32), ([128, XG, D], FP32), ([128, 2, 4, CAP], FP32)]])
        (S,), (xgT, hr, yT) = region("onehot_sources", 2 * QUADS * NT * 64, [
            [([EP, 2, QUADS, NT * 128], BF16)],
            [([128, 2, 2, 128], FP32), ([128, 2, 4, CAP], FP32), ([128, 2, 2, 128], FP32)]])
        (e_src, e_dst, e_f), (Sel, lg, slm, LO, HI) = region("edge_rows", 5 * GE, [
            [([GROUPS, GE], I32), ([GROUPS, GE], I32), ([GROUPS, 3, GE], FP32)],
            [([NP, TOPK, NT, EXPERTS], FP32), ([NP, NT, EXPERTS], FP32), ([NP, NT, EXPERTS], FP32),
             ([NP, TOPK * NT, 128], FP16), ([NP, TOPK * NT, ALL_PAIRS], FP16)]])
        (xn,), (hT,) = region("xn_or_hT", NT * D, [[([NP, NT, D], FP32)], [([128, 2, NODES], FP32)]])
        (nT,), (ocmp,) = region("nT_then_overflow", 2 * OVER_PAIRS * EXPERTS, [
            [([128, 2, NODES], FP32)], [([1, 2 * OVER_PAIRS, EXPERTS], FP32)]])
        fb1s = sb("fb1s", [EXPERTS, HID])
        fb2s = sb("fb2s", [EXPERTS, D])
        (xw,), (sly, cnt, cnt_i, blk_i, ov, cum, dlt) = region("xw_then_slots", NT * D, [
            [([NP, NT, D], FP32)],
            [([NP, TOPK, NT, EXPERTS], FP32), ([NP, EXPERTS], FP32), ([NP, EXPERTS], I32), ([NP, EXPERTS], I32),
             ([NP, EXPERTS], FP32), ([NP, EXPERTS], FP32), ([NP, EXPERTS], FP32)]])
        x1 = xs
        yg = w1r[:, 0:2, :, :].rearrange("p a b c -> p (a b c)")[0:NP, 0:TOPK * NT * D]
        os = w2r[:, 0, :, :].rearrange("p a b -> p (a b)")[0:NP, 0:NT * D]
        acc = w2r[:, 1, :, :].rearrange("p a b -> p (a b)")[0:NP, 0:NT * D]

        ps = [ctx.enter_context(nc.psum_tensor(f"bank{i}", [128, 512], FP32)) for i in range(8)]

        s_ed = sem("edges_loaded")
        s_x = sem("x_loaded")
        s_par = sem("gnn_weights_loaded")
        s_vec = sem("vectors_loaded")
        s_fb = sem("expert_biases_loaded")
        s_rt = sem("router_loaded")
        s_eps = sem("eps_loaded")
        s_pool = sem("pool_step")
        s_cst = sem("constants_made")
        s_at0 = sem("diagonal_made")
        s_dve = sem("dve_step")
        s_efs = sem("fields_copied")
        s_zero = sem("zeros_made")
        s_fill = sem("overflow_rows_filled")
        s_ef = sem("edge_fields_ready")
        s_et = sem("edge_fields_transposed")
        s_ctl = sem("rounds_ready")
        s_var = sem("variance_ready")
        s_std = sem("deviation_ready")
        s_xn = sem("normed_ready")
        s_vt = sem("vectors_transposed")
        s_vc = sem("vectors_copied")
        s_nt = sem("normed_transposed")
        s_ntc = sem("normed_transpose_copied")
        s_xw = sem("xw_done")
        s_xwc = sem("xw_copied")
        s_oh = sem("onehots_ready")
        s_aw = sem("window_done")
        s_awc = sem("window_copied")
        s_at = sem("window_added")
        s_h = sem("h_done")
        s_hc = sem("h_copied")
        s_bn = sem("norm_factors_ready")
        s_hn = sem("h_normed")
        s_bt = sem("back_transposed")
        s_x1 = sem("x1_ready")
        s_bi = sem("expert_bias_transposed")
        s_bic = sem("expert_bias_copied")
        s_xfd = sem("xf_stored")
        s_lg = sem("logits_done")
        s_lgc = sem("logits_copied")
        s_ld = sem("logit_gap_ready")
        s_le = sem("gap_exp_ready")
        s_m = sem("choice_mask_ready")
        s_rk = sem("ranks_done")
        s_lh = sem("slot_onehots_ready")
        s_ix = sem("token_table_done")
        s_ixc = sem("token_table_copied")
        s_ovr = sem("overflow_table_ready")
        s_w1 = [sem(f"w1_loaded{s}") for s in range(RING)]
        s_w2 = [sem(f"w2_loaded{s}") for s in range(RING)]
        s_idn = sem("index_copied")
        s_xg = [sem(f"rows_gathered{s}") for s in range(XG)]
        s_xt = sem("rows_transposed")
        s_xtc = sem("rows_transpose_copied")
        s_g1 = sem("hidden_done")
        s_ha = sem("hidden_biased")
        s_hr = sem("hidden_ready")
        s_g2 = sem("result_done")
        s_ya = sem("result_biased")
        s_yt = sem("result_transposed")
        s_yc = sem("result_copied")
        s_ys = [sem(f"result_stored{s}") for s in range(XG)]
        s_yo = sem("overflow_result_stored")
        s_yg = sem("token_results_gathered")
        s_o = sem("output_ready")
        s_out = sem("output_stored")

        block = ctx.enter_context(nc.Block())

        MAIN_X0, MAIN_W0 = PAIRS // XG, PAIRS // RING
        over_slot = 0

        @block.sync
        def _(sp):
            sp.dma_start(e_dst[:, :], dst.rearrange("(g e) -> g e", g=GROUPS)).then_inc(s_ed, 16)
            sp.dma_start(e_src[:, :], src.rearrange("(g e) -> g e", g=GROUPS)).then_inc(s_ed, 16)
            sp.dma_start(e_f[:, 2, :], ew.rearrange("(g e) -> g e", g=GROUPS)).then_inc(s_ed, 16)
            sp.dma_start(xs[:, :, :], x.rearrange("(p t) d -> p t d", t=NT)).then_inc(s_x, 16)
            sp.dma_start(epsb[:, :], eps.rearrange("(a b) -> a b", a=1).to_broadcast([128, 1])).then_inc(s_eps, 16)
            sp.dma_start(w1g[:, :, :], W1.rearrange("(k p) f -> p k f", k=2)).then_inc(s_par, 16)
            for n, v in enumerate((b1, g1, be1, b2, g2, be2)):
                sp.dma_start(vec[2 * n:2 * n + 2, :], v.rearrange("(o p) -> o p", o=2)).then_inc(s_vec, 16)
            sp.dma_start(w2g[:, :, :], W2.rearrange("(k p) f -> p k f", k=2)).then_inc(s_par, 16)
            sp.dma_start(wrs[:, :, :], Wr.rearrange("(k p) f -> p k f", k=2)).then_inc(s_rt, 16)
            sp.dma_start(brs[:, :], br.rearrange("(a n) -> a n", a=1)).then_inc(s_rt, 16)
            sp.dma_start(fb1s[:, :], fb1).then_inc(s_fb, 16)
            sp.dma_start(fb2s[:, :], fb2).then_inc(s_fb, 16)

            f1 = F1.rearrange("e (p k) f -> p e (k f)", k=2)
            f2 = F2.rearrange("e (p j) f -> p e (j f)", j=4)
            for s in range(RING):
                sp.dma_start(w1r[:, s, :, :], f1[:, 2 * s:2 * s + 2, :]).then_inc(s_w1[s], 16)
                sp.dma_start(w2r[:, s, :, :], f2[:, 2 * s:2 * s + 2, :]).then_inc(s_w2[s], 16)
            with sp.Fori(1, PAIRS // RING) as i:
                for s in range(RING):
                    c = i * RING + s
                    sp.wait_ge(s_g1, (c - RING + 1) * 2)
                    sp.dma_start(w1r[:, s, :, :], f1[:, bass.ds(c * 2, 2), :]).then_inc(s_w1[s], 16)
                    sp.wait_ge(s_g2, (c - RING + 1) * 2)
                    sp.dma_start(w2r[:, s, :, :], f2[:, bass.ds(c * 2, 2), :]).then_inc(s_w2[s], 16)

            sp.wait_ge(s_ovr, 1)
            with sp.Fori(0, OVER_PAIRS) as j:
                used = sp.value_load(oflag[0:1, bass.ds(j, 1)], min_val=0, max_val=1)
                with sp.If(used):
                    sp.wait_ge(s_g1, (j + PAIRS) * 2)
                    sp.wait_ge(s_g2, (j + PAIRS) * 2)
                    for half in range(2):
                        e = sp.value_load(oexp[0:1, bass.ds(j * 2 + half, 1)], min_val=0, max_val=EXPERTS - 1)
                        sp.dma_start(w1r[:, over_slot, half, :], f1[:, bass.ds(e, 1), :].rearrange("p a f -> p (a f)")).then_inc(s_w1[over_slot], 16)
                        sp.dma_start(w2r[:, over_slot, half, :], f2[:, bass.ds(e, 1), :].rearrange("p a f -> p (a f)")).then_inc(s_w2[over_slot], 16)
                    sp.nop()

            sp.wait_ge(s_o, 1)
            sp.dma_start(out.rearrange("(p t) d -> p (t d)", t=NT), os).then_inc(s_out, 16)
            sp.wait_ge(s_out, 16)

        @block.gpsimd
        def _(pool):
            steps = [0]

            def link(ins):
                steps[0] += 1
                ins.then_inc(s_pool, 1)
                pool.wait_ge(s_pool, steps[0])

            pool.iota(iota_src[:, :, :], pattern=[[1, NT], [NT, 128]], base=0, channel_multiplier=0,
                      allow_small_or_imprecise_dtypes=True)
            pool.iota(iota_c[:, :], pattern=[[1, 128]], base=0, channel_multiplier=0,
                      allow_small_or_imprecise_dtypes=True).then_inc(s_cst, 1)
            link(pool.memset(ident[:, :], 0.0))
            pool.affine_select(out=ident[:, :], in_=ident[:, :], compare_op=ALU.not_equal, fill=1.0, base=0,
                               pattern=[[-1, 128]], channel_multiplier=1).then_inc(s_cst, 1)
            pool.iota(w64[:, :, :], pattern=[[WIN, ROUNDS], [0, GROUPS]], base=0, channel_multiplier=0,
                      allow_small_or_imprecise_dtypes=True).then_inc(s_cst, 1)
            link(pool.memset(AT[:, :, :], 0.0))
            link(pool.affine_select(out=AT[:, :, :], in_=AT[:, :, :], compare_op=ALU.not_equal, fill=1.0, base=0,
                                    pattern=[[1, NT], [-1, AT_W]], channel_multiplier=NT))
            pool.wait_ge(s_eps, 16)
            link(pool.tensor_scalar(epsb[:, :], epsb[:, :], 1.0, None, ALU.add))
            pool.tensor_scalar(AT[:, :, :], AT[:, :, :], epsb[:, 0:1], None, ALU.mult).then_inc(s_at0, 1)

            def more_constants():
                pool.memset(zero[:, :], 0.0).then_inc(s_zero, 1)
                link(pool.memset(tri[:, :], 1.0))
                pool.affine_select(out=tri[:, :], in_=tri[:, :], compare_op=ALU.is_gt, fill=0.0, base=0,
                                   pattern=[[1, NP]], channel_multiplier=-1)
                pool.memset(ones_b[:, :], 1.0)
                pool.memset(ones_r[:, :], 1.0)
                pool.iota(e64[:, :], pattern=[[CAP, EXPERTS]], base=0, channel_multiplier=0,
                          allow_small_or_imprecise_dtypes=True)
                pool.iota(tok[:, :], pattern=[[1, NT]], base=0, channel_multiplier=NT,
                          allow_small_or_imprecise_dtypes=True)
                pool.iota(bi[:, :], pattern=[[1, 2 * OVER_PAIRS]], base=0, channel_multiplier=0,
                          allow_small_or_imprecise_dtypes=True)
                pool.iota(pi2[:, :], pattern=[[2, OVER_PAIRS]], base=0, channel_multiplier=0,
                          allow_small_or_imprecise_dtypes=True).then_inc(s_cst, 1)

            more_constants()
            pool.wait_ge(s_ctl, 1)
            pool.wait_ge(s_at0, 1)

            def add_window(it, buf):
                pool.wait_ge(s_awc, it + 1)
                base = pool.value_load(bases[0:1, bass.ds(it, 1)], min_val=0, max_val=NODES - 1)
                win = AT[:, :, bass.ds(base, WIN)]
                pool.tensor_tensor(win, win, AWs[:, buf, :, :], ALU.add).then_inc(s_at, 1)

            add_window(0, 0)
            pool.wait_ge(s_at, 1)
            add_window(1, 1)
            with pool.Fori(1, GROUPS // 2) as i:
                for buf in range(2):
                    pool.wait_ge(s_at, i * 2 + buf)
                    add_window(i * 2 + buf, buf)
            with pool.Fori(1, ROUNDS) as r:
                more = pool.value_load(flags[0:1, bass.ds(r, 1)], min_val=0, max_val=1)
                with pool.If(more):
                    with pool.Fori(0, GROUPS // 2) as i:
                        for buf in range(2):
                            it = r * GROUPS + i * 2 + buf
                            pool.wait_ge(s_at, it)
                            add_window(it, buf)
                    pool.nop()

            def copy_index(c, s):
                pool.tensor_copy(idn[:, s:s + 1], idx[:, bass.ds(c, 1)]).then_inc(s_idn, 1)

            def gather(s, xslot):
                pool.indirect_dma_start(out=xg[:, xslot, :], out_offset=None, in_=xf_dram,
                                        in_offset=bass.IndirectOffsetOnAxis(ap=idn[:, s:s + 1], axis=0),
                                        bounds_check=NODES - 1).then_inc(s_xg[xslot], 16)

            def step(c, s):
                if not isinstance(c, int) or c >= XG:
                    pool.wait_ge(s_xt, c - XG + 1)
                pool.wait_ge(s_idn, c + 1)
                copy_index(c + 1, (s + 1) % RING)
                gather(s, s % XG)

            pool.wait_ge(s_ixc, 1)
            copy_index(0, 0)
            pool.wait_ge(s_xfd, 16)
            for c in range(RING):
                step(c, c)
            with pool.Fori(1, PAIRS // RING) as i:
                for s in range(RING):
                    step(i * RING + s, s)
            pool.wait_ge(s_ovr, 1)
            with pool.Fori(0, OVER_PAIRS) as j:
                used = pool.value_load(oflag[0:1, bass.ds(j, 1)], min_val=0, max_val=1)
                with pool.If(used):
                    pool.wait_ge(s_xt, j + PAIRS)
                    copy_index(j + PAIRS, over_slot)
                    pool.wait_ge(s_idn, j + PAIRS + 2)
                with pool.If(used):
                    gather(over_slot, over_slot)
                    pool.wait_ge(s_yo, (j + 1) * 16)
                    pool.nop()
            pool.wait_ge(s_fill, 16)
            for s in range(XG):
                pool.wait_ge(s_ys[s], 16 * MAIN_X0)
            for m in range(TOPK * NT):
                pool.indirect_dma_start(out=yg[:, m * D:(m + 1) * D], out_offset=None, in_=y_dram,
                                        in_offset=bass.IndirectOffsetOnAxis(ap=sli[:, m:m + 1], axis=0),
                                        bounds_check=ALL_PAIRS * 128 - 1).then_inc(s_yg, 16)

        @block.scalar
        def _(act):
            act.wait_ge(s_var, 1)
            act.activation(nrm[0:NP, 1, :], nrm[0:NP, 0, :], ACT.Sqrt).then_inc(s_std, 1)
            act.wait_ge(s_vt, 1)
            act.activation(vecT[:, :], ps[7][:, 0:NVEC], ACT.Copy).then_inc(s_vc, 1)
            for t in range(NT):
                act.wait_ge(s_nt, t + 1)
                act.activation(nT[:, :, t * NP:(t + 1) * NP],
                               ps[2 + t % 2][:, 0:2 * NP].rearrange("p (k n) -> p k n", k=2), ACT.Copy).then_inc(s_ntc, 1)
            for t in range(NT):
                act.wait_ge(s_xw, t + 1)
                act.activation(xw[:, t, :], ps[4 + t % 2][0:NP, 0:D], ACT.Copy).then_inc(s_xwc, 1)
            for j in range(6):
                act.wait_ge(s_bi, j + 1)
                dstp = b1T[:, :, j] if j < 4 else b2T[:, :, j - 4]
                act.activation(dstp, ps[6][:, j * EXPERTS:(j + 1) * EXPERTS], ACT.Copy).then_inc(s_bic, 1)
            act.wait_ge(s_zero, 1)
            act.dma_start(y_dram[PAIRS * 128:ALL_PAIRS * 128, :].rearrange("(p a) d -> p a d", a=OVER_PAIRS),
                          zero[:, :].unsqueeze(1).to_broadcast([128, OVER_PAIRS, D])).then_inc(s_fill, 16)
            act.wait_ge(s_ctl, 1)

            def copy_window(it, buf):
                act.wait_ge(s_aw, it + 1)
                act.activation(AWs[:, buf, :, :], ps[buf][:, 0:NT * WIN].rearrange("p (s w) -> p s w", s=NT),
                               ACT.Copy).then_inc(s_awc, 1)

            copy_window(0, 0)
            copy_window(1, 1)
            with act.Fori(1, GROUPS // 2) as i:
                for buf in range(2):
                    act.wait_ge(s_at, i * 2 + buf - 1)
                    copy_window(i * 2 + buf, buf)
            with act.Fori(1, ROUNDS) as r:
                more = act.value_load(flags[0:1, bass.ds(r, 1)], min_val=0, max_val=1)
                with act.If(more):
                    with act.Fori(0, GROUPS // 2) as i:
                        for buf in range(2):
                            it = r * GROUPS + i * 2 + buf
                            act.wait_ge(s_at, it - 1)
                            copy_window(it, buf)
                    act.nop()

            for layer in range(2):
                bank0 = 4 - 4 * layer
                for o in range(2):
                    for c, (a, b) in enumerate(CHUNKS):
                        act.wait_ge(s_h, 4 * layer + 2 * o + c + 1)
                        act.activation(hT[:, o, a:b], ps[bank0 + 2 * o + c][:, 0:b - a], ACT.Identity,
                                       bias=vecT[:, 6 * layer + o:6 * layer + o + 1]).then_inc(s_hc, 1)
                    act.wait_ge(s_var, 2 + 2 * layer + o)
                    act.activation(nrm[:, 1, o:o + 1], nrm[:, 0, o:o + 1], ACT.Sqrt).then_inc(s_std, 1)
                act.wait_ge(s_bn, 2 * layer + 2)
                act.activation((nT, hT)[layer][:, 1, :], hT[:, 1, :], ACT.Identity, bias=nrm[:, 5, 1:2],
                               scale=nrm[:, 4, 1:2]).then_inc(s_hn, 1)
            act.wait_ge(s_var, 6)
            act.activation(nrm[0:NP, 1, :], nrm[0:NP, 0, :], ACT.Sqrt).then_inc(s_std, 1)
            act.wait_ge(s_xn, 2 * NT)
            act.dma_start(xf_dram.rearrange("(p t) d -> p (t d)", t=NT), xn[:, :, :].rearrange("p t d -> p (t d)")).then_inc(s_xfd, 16)
            for t in range(NT):
                act.wait_ge(s_nt, NT + t + 1)
                act.activation(nT[:, :, t * NP:(t + 1) * NP],
                               ps[t % 2][:, 0:2 * NP].rearrange("p (k n) -> p k n", k=2), ACT.Copy).then_inc(s_ntc, 1)
            act.wait_ge(s_lg, 1)
            act.activation(lg[:, :, :], ps[3][0:NP, 0:NT * EXPERTS].rearrange("p (t e) -> p t e", t=NT), ACT.Copy).then_inc(s_lgc, 1)
            act.wait_ge(s_ld, 1)
            act.activation(gt[:, 1, :], gt[:, 0, :], ACT.Exp).then_inc(s_le, 1)

            def copy_rows(c, par):
                act.wait_ge(s_xt, c + 1)
                act.activation(xgT[:, par, :, :], ps[par][:, 0:256].rearrange("p (k n) -> p k n", k=2),
                               ACT.Copy).then_inc(s_xtc, 1)

            def relu(c, half):
                act.wait_ge(s_ha, c * 2 + half + 1)
                act.activation(hr[:, half, :, :], hb[:, half, :, :], ACT.Relu).then_inc(s_hr, 1)

            def copy_result(c, par, slot):
                act.wait_ge(s_yt, c + 1)
                act.activation(ys[:, slot, :], ps[6 + par][:, 0:D], ACT.Copy).then_inc(s_yc, 1)

            def store_result(c, slot, done):
                act.wait_ge(s_yc, c + 1)
                act.dma_start(y_dram[bass.ds(c * 128, 128), :], ys[:, slot, :]).then_inc(done, 16)

            def step(c, s, ring_turn):
                static = isinstance(c, int)
                if not static or c >= 2:
                    act.wait_ge(s_g1, (c - 1) * 2)
                copy_rows(c, s % 2)
                if not static or c >= 2:
                    store_result(c - 2, (s - 2) % XG, s_ys[(s - 2) % XG])
                for half in range(2):
                    if not static or c >= 1:
                        act.wait_ge(s_g2, c * 2 + half - 1)
                    relu(c, half)
                if not static or c >= 1:
                    if not static or c > XG:
                        act.wait_ge(s_ys[(s - 1) % XG], ring_turn)
                    copy_result(c - 1, (s - 1) % 2, (s - 1) % XG)

            for c in range(RING):
                step(c, c, 16 * ((c - 1) // XG))
            with act.Fori(1, PAIRS // RING) as i:
                for s in range(RING):
                    step(i * RING + s, s, (i * (RING // XG) + (s - 1) // XG) * 16)
            store_result(PAIRS - 2, (PAIRS - 2) % XG, s_ys[(PAIRS - 2) % XG])
            act.wait_ge(s_ys[(PAIRS - 1) % XG], 16 * (MAIN_X0 - 1))
            copy_result(PAIRS - 1, (PAIRS - 1) % 2, (PAIRS - 1) % XG)
            store_result(PAIRS - 1, (PAIRS - 1) % XG, s_ys[(PAIRS - 1) % XG])

            act.wait_ge(s_ovr, 1)
            act.wait_ge(s_fill, 16)
            act.wait_ge(s_ys[over_slot], 16 * MAIN_X0)
            with act.Fori(0, OVER_PAIRS) as j:
                used = act.value_load(oflag[0:1, bass.ds(j, 1)], min_val=0, max_val=1)
                with act.If(used):
                    c = j + PAIRS
                    act.wait_ge(s_yt, c)
                    copy_rows(c, 0)
                    relu(c, 0)
                    relu(c, 1)
                    copy_result(c, 0, over_slot)
                    store_result(c, over_slot, s_yo)
                    act.nop()

        @block.vector
        def _(dve):
            steps = [0]

            def link(ins):
                steps[0] += 1
                ins.then_inc(s_dve, 1)
                dve.wait_ge(s_dve, steps[0])

            def rsqrt(p, n, count):
                v, sd, r, t = (nrm[0:p, k, n] for k in range(4))
                dve.wait_ge(s_std, count)
                link(dve.reciprocal(r, sd))
                link(dve.tensor_tensor(t, r, r, ALU.mult))
                link(dve.scalar_tensor_tensor(out=t, in0=t, scalar=-0.5, in1=v, op0=ALU.mult, op1=ALU.mult))
                link(dve.scalar_tensor_tensor(out=r, in0=t, scalar=1.5, in1=r, op0=ALU.add, op1=ALU.mult))

            dve.wait_ge(s_ed, 48)
            dve.tensor_copy(e_f[:, 0, :], e_src[:, :])
            link(dve.tensor_copy(e_f[:, 1, :], e_dst[:, :]))
            dve.tensor_reduce(dlo[:, 1:2], e_f[:, 1, :], AX.X, ALU.max)
            link(dve.tensor_reduce(dlo[:, 0:1], e_f[:, 1, :], AX.X, ALU.min))
            dve.tensor_tensor(dlo[:, 2:3], dlo[:, 1:2], dlo[:, 0:1], ALU.subtract)
            dve.tensor_scalar(e_f[:, 1, :], e_f[:, 1, :], dlo[:, 0:1], None, ALU.subtract).then_inc(s_ef, 1)
            dve.wait_ge(s_x, 16)
            for t in range(NT):
                ins = dve.bn_stats(st[0:NP, t, :], xs[:, t, :])
            link(ins)
            for t in range(NT):
                ins = dve.bn_aggr(mv[0:NP, t, :], st[0:NP, t, :])
            link(ins)
            dve.tensor_scalar(nrm[0:NP, 0, :], mv[0:NP, :, 1], EPS, None, ALU.add).then_inc(s_var, 1)
            dve.wait_ge(s_et, 1)
            et = ps[6][0:EP, 0:3 * QUADS * GROUPS].rearrange("p (c g) -> p g c", g=GROUPS)
            link(dve.tensor_copy(EF[:, :, 0:3 * QUADS], et))
            w = [EF[:, :, (2 + k) * QUADS:(3 + k) * QUADS] for k in range(PARTS)]
            wbv = wb[:, :].rearrange("p (g q) -> p g q", g=GROUPS)
            for k in range(1, PARTS):
                link(dve.tensor_copy(wbv, w[k - 1]))
                link(dve.tensor_tensor(w[k], w[k - 1], wbv, ALU.subtract))
            link(dve.tensor_copy(drow[:, :], ps[7][0:1, 64:64 + 2 * GROUPS]))
            link(dve.tensor_reduce(span[:, :], drow[0:1, GROUPS:2 * GROUPS], AX.X, ALU.max))
            dve.wait_ge(s_cst, 3)
            dve.tensor_scalar(flags[:, :], w64[:, :, 0], span[0:1, 0:1], None, ALU.is_le)
            link(dve.tensor_tensor(bases_f[:, :, :], w64[:, :, :],
                                   drow[0:1, 0:GROUPS].unsqueeze(1).to_broadcast([1, ROUNDS, GROUPS]), ALU.add))
            dve.tensor_scalar(bases[:, :], bases_f[:, :, :].rearrange("p r g -> p (r g)"), float(NODES - 1), None,
                              ALU.min).then_inc(s_ctl, 1)
            rsqrt(NP, slice(0, NT), 1)
            for t in range(NT):
                dve.tensor_scalar(xn[:, t, :], xs[:, t, :], mv[0:NP, t, 0:1], nrm[0:NP, 2, t:t + 1],
                                  ALU.subtract, ALU.mult).then_inc(s_xn, 1)
            dve.wait_ge(s_ctl, 1)

            def onehots(buf):
                for q in range(QUADS):
                    f = [EFs[:, buf * 5 * QUADS + k * QUADS + q:buf * 5 * QUADS + k * QUADS + q + 1] for k in range(5)]
                    dve.tensor_scalar(S[:, buf, q, :], iota_src[0:EP, :, :].rearrange("p t n -> p (t n)"), f[0], None, ALU.is_equal)
                    for k in range(PARTS):
                        ins = dve.tensor_scalar(Dw[:, buf, q, k, :], iota_c[0:EP, 0:WIN], f[1], f[2 + k],
                                                ALU.is_equal, ALU.mult)
                ins.then_inc(s_oh, 1)

            def two_groups(r, i):
                for buf in range(2):
                    it = r * GROUPS + i * 2 + buf
                    first = isinstance(it, int) and it < 2
                    fields = EFs[:, buf * 5 * QUADS:(buf + 1) * 5 * QUADS]
                    dve.wait_ge(s_ef, r + 1)
                    if not first:
                        dve.wait_ge(s_oh, it - 1)
                    dve.tensor_copy(fields, EF[:, bass.ds(i * 2 + buf, 1), :].rearrange("p g c -> p (g c)")).then_inc(s_efs, 1)
                    if not first:
                        dve.wait_ge(s_aw, it - 1)
                    dve.wait_ge(s_efs, it + 1)
                    onehots(buf)

            two_groups(0, 0)
            with dve.Fori(1, GROUPS // 2) as i:
                two_groups(0, i)
            with dve.Fori(1, ROUNDS) as r:
                more = dve.value_load(flags[0:1, bass.ds(r, 1)], min_val=0, max_val=1)
                with dve.If(more):
                    dve.tensor_scalar(EF[:, :, QUADS:2 * QUADS], EF[:, :, QUADS:2 * QUADS], float(WIN), None,
                                      ALU.subtract).then_inc(s_ef, 1)
                    with dve.Fori(0, GROUPS // 2) as i:
                        two_groups(r, i)
                    dve.nop()

            for layer in range(2):
                for o in range(2):
                    for c, (a, b) in enumerate(CHUNKS):
                        dve.wait_ge(s_hc, 4 * layer + 2 * o + c + 1)
                        ins = dve.bn_stats(st[:, 2 * o + c, :], hT[:, o, a:b])
                    link(ins)
                    link(dve.bn_aggr(mv[:, o, :], st[:, 2 * o:2 * o + 2, :]))
                    dve.tensor_scalar(nrm[:, 0, o:o + 1], mv[:, o, 1:2], EPS, None, ALU.add).then_inc(s_var, 1)
                    rsqrt(128, slice(o, o + 1), 2 + 2 * layer + o)
                    if layer == 0 and o == 0:
                        dve.wait_ge(s_vc, 1)
                    gain, shift = (vecT[:, 6 * layer + 2 * k + o:6 * layer + 2 * k + o + 1] for k in (1, 2))
                    link(dve.tensor_tensor(nrm[:, 4, o:o + 1], nrm[:, 2, o:o + 1], gain, ALU.mult))
                    link(dve.tensor_tensor(nrm[:, 3, o:o + 1], nrm[:, 4, o:o + 1], mv[:, o, 0:1], ALU.mult))
                    dve.tensor_tensor(nrm[:, 5, o:o + 1], shift, nrm[:, 3, o:o + 1], ALU.subtract).then_inc(s_bn, 1)
                    if o == 0:
                        dve.wait_ge(s_bn, 2 * layer + 1)
                        dve.tensor_scalar((nT, hT)[layer][:, 0, :], hT[:, 0, :], nrm[:, 4, 0:1], nrm[:, 5, 0:1],
                                          ALU.mult, ALU.add).then_inc(s_hn, 1)
            for t in range(NT):
                dve.wait_ge(s_bt, t + 1)
                dve.tensor_tensor(x1[:, t, :], ps[4 + t % 4][0:NP, 0:D], xs[:, t, :], ALU.add).then_inc(s_x1, 1)
                dve.wait_ge(s_x1, t + 1)
                ins = dve.bn_stats(st[0:NP, t, :], x1[:, t, :])
            link(ins)
            for t in range(NT):
                ins = dve.bn_aggr(mv[0:NP, t, :], st[0:NP, t, :])
            link(ins)
            dve.tensor_scalar(nrm[0:NP, 0, :], mv[0:NP, :, 1], EPS, None, ALU.add).then_inc(s_var, 1)
            rsqrt(NP, slice(0, NT), 6)
            for t in range(NT):
                dve.tensor_scalar(xn[:, t, :], x1[:, t, :], mv[0:NP, t, 0:1], nrm[0:NP, 2, t:t + 1],
                                  ALU.subtract, ALU.mult).then_inc(s_xn, 1)

            dve.wait_ge(s_lgc, 1)
            for t in range(NT):
                ins = dve.max(m8[:, t, :], lg[:, t, :])
            link(ins)
            for t in range(NT):
                ins = dve.max_index(i8[:, t, :], m8[:, t, :], lg[:, t, :])
            dve.tensor_tensor(gt[:, 0, :], m8[:, :, 1], m8[:, :, 0], ALU.subtract).then_inc(s_ld, 1)
            dve.wait_ge(s_ld, 1)
            link(dve.tensor_copy(ixf[:, :, :], i8[:, :, 0:TOPK].rearrange("p t k -> p k t")))
            dve.wait_ge(s_cst, 4)
            experts = iota_c[0:NP, 0:EXPERTS].unsqueeze(1).to_broadcast([NP, TOPK * NT, EXPERTS])
            link(dve.tensor_tensor(Sel[:, :, :, :].rearrange("p k t e -> p (k t) e"), experts,
                                   ixf[:, :, :].rearrange("p k t -> p (k t)").unsqueeze(2).to_broadcast([NP, TOPK * NT, EXPERTS]),
                                   ALU.is_equal))
            dve.tensor_tensor(Mb[:, :, :], Sel[:, 0, :, :], Sel[:, 1, :, :], ALU.add).then_inc(s_m, 1)
            dve.wait_ge(s_rk, 1)
            link(dve.tensor_scalar(cnt_i[:, :], ps[4][0:NP, 0:EXPERTS], float(CAP - 1), None, ALU.add))
            link(dve.tensor_scalar(blk_i[:, :], cnt_i[:, :], 6, None, ALU.arith_shift_right))
            link(dve.tensor_scalar(ov[:, :], blk_i[:, :], 1.0, 0.0, ALU.subtract, ALU.max))
            link(dve.memset(cnt[:, :], 0.0))
            link(dve.tensor_tensor_scan(cum[:, :], ov[:, :], cnt[:, :], 0.0, ALU.add, ALU.add))
            link(dve.tensor_tensor(dlt[:, :], cum[:, :], ov[:, :], ALU.subtract))
            link(dve.tensor_scalar(dlt[:, :], dlt[:, :], float(CAP), float((EXPERTS - 1) * CAP), ALU.mult, ALU.add))
            link(dve.tensor_tensor(dlt[:, :], dlt[:, :], e64[:, :], ALU.subtract))
            rank = ps[7][0:NP, 0:NT * EXPERTS].rearrange("p (t e) -> p t e", t=NT)

            def over_tiles(a):
                return a.unsqueeze(1).to_broadcast([NP, NT, EXPERTS])

            link(dve.scalar_tensor_tensor(out=slm[:, :, :], in0=rank, scalar=float(CAP), in1=over_tiles(dlt[:, :]),
                                          op0=ALU.is_ge, op1=ALU.mult))
            link(dve.tensor_tensor(slm[:, :, :], slm[:, :, :], over_tiles(e64[:, :]), ALU.add))
            link(dve.tensor_tensor(slm[:, :, :], slm[:, :, :], rank, ALU.add))
            for k in range(TOPK):
                ins = dve.tensor_tensor(sly[:, k, :, :], slm[:, :, :], Sel[:, k, :, :], ALU.mult)
            link(ins)
            link(dve.tensor_reduce(slf[:, :], sly[:, :, :, :].rearrange("p k t e -> p (k t) e"), AX.X, ALU.add))
            link(dve.tensor_copy(sli[:, :], slf[:, :]))
            dve.tensor_scalar(lohi[:, 0, :], sli[:, :], 127, None, ALU.bitwise_and)
            link(dve.tensor_scalar(lohi[:, 1, :], sli[:, :], 7, None, ALU.logical_shift_right))
            link(dve.tensor_copy(lhf[:, :, :], lohi[:, :, :]))
            for m in range(TOPK * NT):
                dve.tensor_scalar(LO[:, m, :], iota_c[0:NP, :], lhf[:, 0, m:m + 1], None, ALU.is_equal)
                dve.tensor_scalar(HI[:, m, :], iota_c[0:NP, 0:ALL_PAIRS], lhf[:, 1, m:m + 1],
                                  tok[:, m % NT:m % NT + 1], ALU.is_equal, ALU.mult).then_inc(s_lh, 1)
            dve.wait_ge(s_ix, 1)
            dve.tensor_copy(idx[:, :], ps[5][:, 0:ALL_PAIRS]).then_inc(s_ixc, 1)
            dve.tensor_scalar(oflag[:, :], pi2[:, :], cum[0:1, EXPERTS - 1:EXPERTS], None, ALU.is_lt)
            link(dve.tensor_tensor(ocmp[:, :, :], bi[0:1, :].unsqueeze(2).to_broadcast([1, 2 * OVER_PAIRS, EXPERTS]),
                                   cum[0:1, :].unsqueeze(1).to_broadcast([1, 2 * OVER_PAIRS, EXPERTS]), ALU.is_ge))
            link(dve.tensor_reduce(oexp_f[:, :], ocmp[:, :, :], AX.X, ALU.add))
            dve.tensor_scalar(oexp[:, :], oexp_f[:, :], float(EXPERTS - 1), None, ALU.min).then_inc(s_ovr, 1)
            dve.wait_ge(s_le, 1)
            link(dve.tensor_scalar(gt[:, 2, :], gt[:, 1, :], 1.0, None, ALU.add))
            link(dve.reciprocal(gt[:, 3, :], gt[:, 2, :]))
            link(dve.tensor_tensor(gt[:, 4, :], gt[:, 1, :], gt[:, 3, :], ALU.mult))
            dve.wait_ge(s_bic, 6)

            def bias_result(c, par, bias):
                dve.wait_ge(s_g2, c * 2 + 2)
                dve.tensor_tensor(yT[:, par, :, :].rearrange("p o (h n) -> p h o n", h=2),
                                  ps[4 + par][:, 0:256].rearrange("p (o h n) -> p h o n", o=2, h=2),
                                  bias.unsqueeze(3).to_broadcast([128, 2, 2, CAP]), ALU.add).then_inc(s_ya, 1)

            def bias_hidden(c, half, bias):
                dve.wait_ge(s_g1, c * 2 + half + 1)
                dve.tensor_tensor(hb[:, half, :, :], ps[2 + half][:, 0:4 * CAP].rearrange("p (j n) -> p j n", j=4),
                                  bias.unsqueeze(2).to_broadcast([128, 4, CAP]), ALU.add).then_inc(s_ha, 1)

            def pair_bias2(c):
                return b2T[:, bass.ds(c * 2, 2), :]

            def step(c, s):
                static = isinstance(c, int)
                if not static or c >= 1:
                    if not static or c >= 3:
                        dve.wait_ge(s_yt, c - 2)
                    bias_result(c - 1, (s - 1) % 2, pair_bias2(c - 1))
                for half in range(2):
                    if not static or c >= 1:
                        dve.wait_ge(s_hr, c * 2 + half - 1)
                    bias_hidden(c, half, b1T[:, bass.ds(c * 2 + half, 1), :].rearrange("p a j -> p (a j)"))

            for c in range(RING):
                step(c, c)
            with dve.Fori(1, PAIRS // RING) as i:
                for s in range(RING):
                    step(i * RING + s, s)
            dve.wait_ge(s_yt, PAIRS - 2)
            bias_result(PAIRS - 1, (PAIRS - 1) % 2, pair_bias2(PAIRS - 1))
            with dve.Fori(0, OVER_PAIRS) as j:
                used = dve.value_load(oflag[0:1, bass.ds(j, 1)], min_val=0, max_val=1)
                with dve.If(used):
                    c = j + PAIRS
                    dve.wait_ge(s_yt, c)
                    for half in range(2):
                        e = dve.value_load(oexp[0:1, bass.ds(j * 2 + half, 1)], min_val=0, max_val=EXPERTS - 1)
                        dve.tensor_copy(b1o[:, half, :], b1T[:, bass.ds(e, 1), :].rearrange("p a j -> p (a j)"))
                        ins = dve.tensor_copy(b2o[:, half, :], b2T[:, bass.ds(e, 1), :].rearrange("p a j -> p (a j)"))
                    ins.then_inc(s_vc, 1)
                    dve.wait_ge(s_vc, j + 2)
                    for half in range(2):
                        bias_hidden(c, half, b1o[:, half, :])
                    bias_result(c, 0, b2o[:, :, :])
                    dve.nop()
            dve.wait_ge(s_yg, 16 * TOPK * NT)
            for t in range(NT):
                ins = dve.scalar_tensor_tensor(out=acc[:, t * D:(t + 1) * D], in0=yg[:, t * D:(t + 1) * D],
                                               scalar=gt[:, 3, t:t + 1], in1=x1[:, t, :], op0=ALU.mult, op1=ALU.add)
            link(ins)
            for t in range(NT):
                m = NT + t
                ins = dve.scalar_tensor_tensor(out=os[:, t * D:(t + 1) * D], in0=yg[:, m * D:(m + 1) * D],
                                               scalar=gt[:, 4, t:t + 1], in1=acc[:, t * D:(t + 1) * D],
                                               op0=ALU.mult, op1=ALU.add)
            ins.then_inc(s_o, 1)

        @block.tensor
        def _(pe):
            mm, idt = pe.matmul, ident
            pe.wait_ge(s_cst, 2)
            pe.wait_ge(s_ef, 1)
            for k, col in enumerate((0, 2)):
                pe.transpose(ps[7][0:1, 64 + k * GROUPS:64 + (k + 1) * GROUPS], dlo[:, col:col + 1], idt[0:GROUPS, 0:GROUPS])
            for f in range(3):
                for q in range(QUADS):
                    m = f * QUADS + q
                    ins = pe.transpose(ps[6][0:EP, m * GROUPS:(m + 1) * GROUPS], e_f[:, f, q * EP:(q + 1) * EP],
                                       idt[0:GROUPS, 0:GROUPS])
            ins.then_inc(s_et, 1)
            pe.wait_ge(s_ctl, 1)
            pe.wait_ge(s_vec, 96)
            pe.transpose(ps[7][:, 0:NVEC], vec[:, :], idt[0:NVEC, 0:NVEC]).then_inc(s_vt, 1)
            for t in range(NT):
                pe.wait_ge(s_xn, t + 1)
                if t >= 2:
                    pe.wait_ge(s_ntc, t - 1)
                for k in range(2):
                    ins = pe.transpose(ps[2 + t % 2][:, k * NP:(k + 1) * NP], xn[:, t, k * 128:(k + 1) * 128],
                                       idt[0:NP, 0:NP])
                ins.then_inc(s_nt, 1)
            pe.wait_ge(s_par, 32)
            for t in range(NT):
                pe.wait_ge(s_ntc, t + 1)
                if t >= 2:
                    pe.wait_ge(s_xwc, t - 1)
                for k in range(2):
                    ins = mm(ps[4 + t % 2][0:NP, 0:D], nT[:, k, t * NP:(t + 1) * NP], w1g[:, k, :],
                             start=(k == 0), stop=(k == 1))
                ins.then_inc(s_xw, 1)
            pe.wait_ge(s_fb, 32)
            for j in range(6):
                if j:
                    pe.wait_ge(s_bic, j)
                a = fb1s[:, j:HID:4] if j < 4 else fb2s[:, (j - 4) * 128:(j - 3) * 128]
                pe.transpose(ps[6][:, j * EXPERTS:(j + 1) * EXPERTS], a, idt[0:EXPERTS, 0:EXPERTS]).then_inc(s_bi, 1)

            def group(it, buf):
                pe.wait_ge(s_oh, it + 1)
                for s in range(NT):
                    for q in range(QUADS):
                        for k in range(PARTS):
                            ins = mm(ps[buf][:, s * WIN:(s + 1) * WIN], S[:, buf, q, s * 128:(s + 1) * 128],
                                     Dw[:, buf, q, k, :], start=(q == 0 and k == 0),
                                     stop=(q == QUADS - 1 and k == PARTS - 1))
                ins.then_inc(s_aw, 1)

            group(0, 0)
            group(1, 1)
            with pe.Fori(1, GROUPS // 2) as i:
                for buf in range(2):
                    pe.wait_ge(s_awc, i * 2 + buf - 1)
                    group(i * 2 + buf, buf)
            with pe.Fori(1, ROUNDS) as r:
                more = pe.value_load(flags[0:1, bass.ds(r, 1)], min_val=0, max_val=1)
                with pe.If(more):
                    with pe.Fori(0, GROUPS // 2) as i:
                        for buf in range(2):
                            it = r * GROUPS + i * 2 + buf
                            pe.wait_ge(s_awc, it - 1)
                            group(it, buf)
                    pe.nop()

            pe.wait_ge(s_xwc, NT)
            pe.wait_ge(s_at, GROUPS)
            with pe.Fori(1, ROUNDS) as r:
                more = pe.value_load(flags[0:1, bass.ds(r, 1)], min_val=0, max_val=1)
                with pe.If(more):
                    pe.wait_ge(s_at, (r + 1) * GROUPS)
                    pe.nop()
            for o in range(2):
                for c, (a, b) in enumerate(CHUNKS):
                    for s in range(NT):
                        ins = mm(ps[4 + 2 * o + c][:, 0:b - a], xw[:, s, o * 128:(o + 1) * 128], AT[0:NP, s, a:b],
                                 start=(s == 0), stop=(s == NT - 1))
                    ins.then_inc(s_h, 1)
            pe.wait_ge(s_hn, 2)
            for o in range(2):
                for c, (a, b) in enumerate(CHUNKS):
                    for k in range(2):
                        ins = mm(ps[2 * o + c][:, 0:b - a], w2g[:, k, o * 128:(o + 1) * 128], nT[:, k, a:b],
                                 start=(k == 0), stop=(k == 1))
                    ins.then_inc(s_h, 1)
            pe.wait_ge(s_hn, 4)
            for t in range(NT):
                if t >= 4:
                    pe.wait_ge(s_x1, t - 3)
                for k in range(2):
                    ins = pe.transpose(ps[4 + t % 4][0:NP, k * 128:(k + 1) * 128], hT[:, k, t:NODES:NT], idt[:, :])
                ins.then_inc(s_bt, 1)
            for t in range(NT):
                pe.wait_ge(s_xn, NT + t + 1)
                if t >= 2:
                    pe.wait_ge(s_ntc, NT + t - 1)
                for k in range(2):
                    ins = pe.transpose(ps[t % 2][:, k * NP:(k + 1) * NP], xn[:, t, k * 128:(k + 1) * 128],
                                       idt[0:NP, 0:NP])
                ins.then_inc(s_nt, 1)
            pe.wait_ge(s_rt, 32)
            pe.wait_ge(s_cst, 4)
            for t in range(NT):
                pe.wait_ge(s_ntc, NT + t + 1)
                lgp = ps[3][0:NP, t * EXPERTS:(t + 1) * EXPERTS]
                for k in range(2):
                    mm(lgp, nT[:, k, t * NP:(t + 1) * NP], wrs[:, k, :], start=(k == 0), stop=False)
                ins = mm(lgp, ones_r[:, :], brs[:, :], start=False, stop=True)
            ins.then_inc(s_lg, 1)
            pe.wait_ge(s_m, 1)
            for t in range(NT):
                for u in range(t + 1):
                    mm(ps[7][0:NP, t * EXPERTS:(t + 1) * EXPERTS], ones_b[:, :] if u < t else tri[:, :], Mb[:, u, :],
                       start=(u == 0), stop=(u == t))
            for u in range(NT):
                ins = mm(ps[4][0:NP, 0:EXPERTS], ones_b[:, :], Mb[:, u, :], start=(u == 0), stop=(u == NT - 1))
            ins.then_inc(s_rk, 1)
            for m in range(TOPK * NT):
                pe.wait_ge(s_lh, m + 1)
                ins = mm(ps[5][:, 0:ALL_PAIRS], LO[:, m, :], HI[:, m, :], start=(m == 0), stop=(m == TOPK * NT - 1))
            ins.then_inc(s_ix, 1)

            def rows_T(c, par, slot, gathered):
                pe.wait_ge(s_xg[slot], gathered)
                for k in range(2):
                    ins = pe.transpose(ps[par][:, k * 128:(k + 1) * 128], xg[:, slot, k:D:2], idt[:, :])
                ins.then_inc(s_xt, 1)

            def hidden(half, par, slot):
                for j in range(4):
                    for k in range(2):
                        ins = mm(ps[2 + half][:, j * CAP:(j + 1) * CAP],
                                 w1r[:, slot, half, k * HID + j:(k + 1) * HID:4],
                                 xgT[:, par, k, half * CAP:(half + 1) * CAP], start=(k == 0), stop=(k == 1))
                ins.then_inc(s_g1, 1)

            def result(c, half, par, slot):
                pe.wait_ge(s_hr, c * 2 + half + 1)
                for o in range(2):
                    for j in range(4):
                        ins = mm(ps[4 + par][:, o * 128 + half * CAP:o * 128 + (half + 1) * CAP],
                                 w2r[:, slot, half, j * D + o * 128:j * D + (o + 1) * 128],
                                 hr[:, half, j, :], start=(j == 0), stop=(j == 3))
                ins.then_inc(s_g2, 1)

            def result_T(c, par):
                pe.wait_ge(s_ya, c + 1)
                for o in range(2):
                    ins = pe.transpose(ps[6 + par][:, o * 128:(o + 1) * 128], yT[:, par, o, :], idt[:, :])
                ins.then_inc(s_yt, 1)

            def results(c, s, loads):
                par = s % 2
                pe.wait_ge(s_w2[s], loads)
                if not isinstance(c, int) or c >= 2:
                    pe.wait_ge(s_ya, c - 1)
                for half in range(2):
                    result(c, half, par, s)

            def results_T(c, s):
                if not isinstance(c, int) or c >= 2:
                    pe.wait_ge(s_yc, c - 1)
                result_T(c, s % 2)

            def step(c, s, gathered, loads, loads_before):
                static = isinstance(c, int)
                if not static or c >= 2:
                    pe.wait_ge(s_xtc, c - 1)
                rows_T(c, s % 2, s % XG, gathered)
                if not static or c >= 1:
                    results(c - 1, (s - 1) % RING, loads_before)
                pe.wait_ge(s_w1[s], loads)
                pe.wait_ge(s_xtc, c + 1)
                for half in range(2):
                    if not static or c >= 1:
                        pe.wait_ge(s_ha, c * 2 + half - 1)
                    hidden(half, s % 2, s)
                if not static or c >= 1:
                    results_T(c - 1, (s - 1) % RING)

            pe.wait_ge(s_ixc, 1)
            for c in range(RING):
                step(c, c, 16 * (c // XG + 1), 16, 16)
            with pe.Fori(1, PAIRS // RING) as i:
                for s in range(RING):
                    step(i * RING + s, s, (i * (RING // XG) + s // XG + 1) * 16, (i + 1) * 16,
                         (i + 1) * 16 if s else i * 16)
            results(PAIRS - 1, RING - 1, 16 * MAIN_W0)
            results_T(PAIRS - 1, RING - 1)
            pe.wait_ge(s_ovr, 1)
            with pe.Fori(0, OVER_PAIRS) as j:
                used = pe.value_load(oflag[0:1, bass.ds(j, 1)], min_val=0, max_val=1)
                with pe.If(used):
                    c = j + PAIRS
                    pe.wait_ge(s_yc, c)
                    rows_T(c, 0, over_slot, (j + MAIN_X0 + 1) * 16)
                    pe.wait_ge(s_w1[over_slot], (j * 2 + MAIN_W0 + 2) * 16)
                    pe.wait_ge(s_xtc, c + 1)
                    for half in range(2):
                        hidden(half, 0, over_slot)
                    pe.wait_ge(s_w2[over_slot], (j * 2 + MAIN_W0 + 2) * 16)
                    for half in range(2):
                        result(c, half, 0, over_slot)
                    result_T(c, 0)
                    pe.nop()


_INS = ['x', 'src', 'dst', 'edge_weight', 'L0_gnn_W1', 'L0_gnn_b1', 'L0_gnn_g1', 'L0_gnn_be1', 'L0_gnn_W2',
        'L0_gnn_b2', 'L0_gnn_g2', 'L0_gnn_be2', 'L0_gnn_eps', 'L0_ffn_Wr', 'L0_ffn_br', 'L0_ffn_W1', 'L0_ffn_b1',
        'L0_ffn_W2', 'L0_ffn_b2']


def kernel(**inputs):
    import numpy as np
    import concourse.bacc as bacc
    from concourse import mybir
    from concourse.bass_utils import run_bass_kernel_spmd

    nc = bacc.Bacc("TRN2", target_bir_lowering=False, num_devices=1)
    arrays, args = {}, []
    for name in _INS:
        a = np.ascontiguousarray(inputs[name])
        arrays[f"in_{name}"] = a
        args.append(nc.dram_tensor(f"in_{name}", a.shape, mybir.dt.from_np(a.dtype), kind="ExternalInput").ap())
    args.append(nc.dram_tensor("out_0", (NODES, D), mybir.dt.float32, kind="ExternalOutput").ap())
    gnn_moe(nc, *args)
    r = run_bass_kernel_spmd(nc, [arrays], core_ids=[0])
    return r.results[0]["out_0"]
```

```python
import concourse.bass as bass
from concourse import mybir
from contextlib import ExitStack

FP32 = mybir.dt.float32
BF16 = mybir.dt.bfloat16
FP16 = mybir.dt.float16
I32 = mybir.dt.int32
U32 = mybir.dt.uint32
ALU = mybir.AluOpType
ACT = mybir.ActivationFunctionType
AX = mybir.AxisListType

NODES, EDGES, D, HID, EXPERTS, TOPK = 625, 10000, 256, 512, 64, 2
NT, NP = 5, 125
GROUPS, QUADS, EP = 20, 4, 125
GE = QUADS * EP
WIN = 64
ROUNDS = -(-NODES // WIN)
AT_W = NODES - 1 + WIN
PARTS = 3
CAP = 64
PAIRS = EXPERTS // 2
MAX_OVER = (NODES * TOPK - 2) // CAP
OVER_PAIRS = (MAX_OVER + 1) // 2
ALL_PAIRS = PAIRS + OVER_PAIRS
RING = 8
ROWS = 1 + TOPK * NODES
XG = 4
EPS = 1e-5
C0 = 320
CHUNKS = [(0, C0), (C0, NODES)]
NVEC = 12


def gnn_moe(nc, x, src, dst, ew, W1, b1, g1, be1, W2, b2, g2, be2, eps, Wr, br, F1, fb1, F2, fb2, out):
    ctx = ExitStack()
    with ctx:
        def sb(name, shape, dt=FP32):
            return ctx.enter_context(nc.sbuf_tensor(name, shape, dt))

        def sem(name):
            return ctx.enter_context(nc.semaphore(name))

        def region(name, words, tensors):
            tile = sb(name, [128, words])

            def cut(*wanted):
                at, views = 0, []
                for shape, dt in wanted:
                    count = 1
                    for n in shape[1:]:
                        count *= n
                    size = -(-count * (2 if dt in (BF16, FP16) else 4) // 4)
                    assert at + size <= words, (name, at + size)
                    v = tile[0:shape[0], at:at + size]
                    if dt != FP32:
                        v = v.bitcast(dt)
                    letters = "abcd"[0:len(shape) - 1]
                    v = v.rearrange(f"p ({' '.join(letters)}) -> p {' '.join(letters)}",
                                    **dict(zip(letters, shape[1:])))
                    views.append(v)
                    at += size
                return views

            return [cut(*t) for t in tensors]

        xf_dram = nc.dram_tensor("xf_rows", [ROWS, D], FP32).ap()
        y_dram = nc.dram_tensor("y_rows", [ROWS + ALL_PAIRS * 128, D], FP32).ap()

        w1r = sb("w1_ring", [128, RING, 2, 2 * HID])
        w2r = sb("w2_ring", [128, RING, 2, 4 * D])
        ident = sb("ident", [128, 128])
        iota_src = sb("iota_src", [128, NT, 128], FP16)
        iota_c = sb("iota_c", [128, 128], FP16)
        tri = sb("tri", [NP, NP], BF16)
        ones_b = sb("ones_b", [NP, NP], BF16)
        ones_r = sb("ones_r", [1, NP])
        e64 = sb("e64", [NP, EXPERTS])
        tok = sb("tok", [NP, TOPK * NT])
        spare = sb("spare", [128, ALL_PAIRS])
        dsf = sb("dsf", [128, ALL_PAIRS])
        w64 = sb("w64", [1, ROUNDS, GROUPS])
        bi = sb("bi", [1, 2 * OVER_PAIRS])
        pi2 = sb("pi2", [1, OVER_PAIRS])
        xs = sb("xs", [NP, NT, D])
        AWs = sb("AWs", [128, 2, NT, WIN])
        Dw = sb("Dw", [EP, 2, QUADS, PARTS, WIN], BF16)
        w1g = sb("w1g", [128, 2, D])
        w2g = sb("w2g", [128, 2, D])
        wrs = sb("wrs", [128, 2, EXPERTS])
        brs = sb("brs", [1, EXPERTS])
        vec = sb("vec", [NVEC, 128])
        vecT = sb("vecT", [128, NVEC])
        epsb = sb("epsb", [128, 1])
        dlo = sb("dlo", [GROUPS, 4])
        drow = sb("drow", [1, 2 * GROUPS])
        span = sb("span", [1, 1])
        flags = sb("flags", [1, ROUNDS], I32)
        bases_f = sb("bases_f", [1, ROUNDS, GROUPS])
        bases = sb("bases", [1, ROUNDS * GROUPS], I32)
        wb = sb("wb", [EP, GROUPS * QUADS], BF16)
        EF = sb("EF", [EP, GROUPS, 5 * QUADS])
        EFs = sb("EFs", [EP, 2 * 5 * QUADS])
        st = sb("st", [128, NT, 6])
        mv = sb("mv", [128, NT, 2])
        nrm = sb("nrm", [128, 6, NT])
        b1T = sb("b1T", [128, 4, EXPERTS])
        b1o = sb("b1o", [128, 4, 2])
        m8 = sb("m8", [NP, NT, 8])
        i8 = sb("i8", [NP, NT, 8], U32)
        ixf = sb("ixf", [NP, TOPK, NT])
        gt = sb("gt", [NP, 5, NT])
        Mb = sb("Mb", [NP, NT, EXPERTS], BF16)
        slf = sb("slf", [NP, TOPK * NT])
        sli = sb("sli", [NP, TOPK * NT], U32)
        lohi = sb("lohi", [NP, 2, TOPK * NT], U32)
        lhf = sb("lhf", [NP, 2, TOPK * NT])
        idx = sb("idx", [128, ALL_PAIRS, 2], U32)
        idn = sb("idn", [128, RING, 2], U32)
        done = sb("done", [1, 1])
        oexp_f = sb("oexp_f", [1, 2 * OVER_PAIRS])
        oexp = sb("oexp", [1, 2 * OVER_PAIRS], I32)
        oflag = sb("oflag", [1, OVER_PAIRS], I32)
        (AT,), (xg, ys, hb) = region("adjacency", NT * AT_W, [
            [([128, NT, AT_W], FP32)],
            [([128, XG, D], FP32), ([128, XG, D], FP32), ([128, 4, 128], FP32)]])
        (S,), (xgT, hr, hn) = region("onehot_sources", 2 * QUADS * NT * 64, [
            [([EP, 2, QUADS, NT * 128], BF16)],
            [([128, 2, 2, 128], FP32), ([128, 2, 4, 128], FP32), ([128, 2, HID], FP32)]])
        (e_src, e_dst, e_f), (Sel, lg, slm, LO, HI) = region("edge_rows", 5 * GE, [
            [([GROUPS, GE], I32), ([GROUPS, GE], I32), ([GROUPS, 3, GE], FP32)],
            [([NP, TOPK, NT, EXPERTS], FP32), ([NP, NT, EXPERTS], FP32), ([NP, NT, EXPERTS], FP32),
             ([NP, TOPK * NT, 128], FP16), ([NP, TOPK * NT, ALL_PAIRS], FP16)]])
        (xn,), (hT,) = region("xn_or_hT", NT * D, [[([NP, NT, D], FP32)], [([128, 2, NODES], FP32)]])
        (nT,), (ocmp,), (GT,) = region("nT_then_overflow", 2 * OVER_PAIRS * EXPERTS, [
            [([128, 2, NODES], FP32)], [([1, 2 * OVER_PAIRS, EXPERTS], FP32)], [([EXPERTS, NODES], FP32)]])
        fb1s = sb("fb1s", [EXPERTS, HID])
        fb2s = sb("fb2s", [EXPERTS, D])
        (xw,), (sly, cnt, cnt_i, blk_i, ov, cum, dlt) = region("xw_then_slots", NT * D, [
            [([NP, NT, D], FP32)],
            [([NP, TOPK, NT, EXPERTS], FP32), ([NP, EXPERTS], FP32), ([NP, EXPERTS], I32), ([NP, EXPERTS], I32),
             ([NP, EXPERTS], FP32), ([NP, EXPERTS], FP32), ([NP, EXPERTS], FP32)]])
        x1 = xs
        yg = w1r[:, 0:2, :, :].rearrange("p a b c -> p (a b c)")[0:NP, 0:TOPK * NT * D].rearrange(
            "p (k t d) -> p k t d", k=TOPK, t=NT)
        os, acc = (w2r[:, s, :, :].rearrange("p a b -> p (a b)")[0:NP, 0:NT * D].rearrange("p (t d) -> p t d", t=NT)
                   for s in range(2))

        ps = [ctx.enter_context(nc.psum_tensor(f"bank{i}", [128, 512], FP32)) for i in range(8)]

        s_ed = sem("edges_loaded")
        s_x = sem("x_loaded")
        s_par = sem("gnn_weights_loaded")
        s_vec = sem("vectors_loaded")
        s_fb = sem("expert_biases_loaded")
        s_rt = sem("router_loaded")
        s_eps = sem("eps_loaded")
        s_pool = sem("pool_step")
        s_cst = sem("constants_made")
        s_at0 = sem("diagonal_made")
        s_dve = sem("dve_step")
        s_efs = sem("fields_copied")
        s_ef = sem("edge_fields_ready")
        s_et = sem("edge_fields_transposed")
        s_ctl = sem("rounds_ready")
        s_var = sem("variance_ready")
        s_std = sem("deviation_ready")
        s_xn = sem("normed_ready")
        s_vt = sem("vectors_transposed")
        s_vc = sem("vectors_copied")
        s_nt = sem("normed_transposed")
        s_ntc = sem("normed_transpose_copied")
        s_xw = sem("xw_done")
        s_xwc = sem("xw_copied")
        s_oh = sem("onehots_ready")
        s_aw = sem("window_done")
        s_awc = sem("window_copied")
        s_at = sem("window_added")
        s_h = sem("h_done")
        s_hc = sem("h_copied")
        s_bn = sem("norm_factors_ready")
        s_hn = sem("h_normed")
        s_bt = sem("back_transposed")
        s_x1 = sem("x1_ready")
        s_bi = sem("expert_bias_transposed")
        s_bic = sem("expert_bias_copied")
        s_xfd = sem("xf_stored")
        s_lg = sem("logits_done")
        s_lgc = sem("logits_copied")
        s_ld = sem("logit_gap_ready")
        s_le = sem("gap_exp_ready")
        s_m = sem("choice_mask_ready")
        s_rk = sem("ranks_done")
        s_lh = sem("slot_onehots_ready")
        s_ix = sem("token_table_done")
        s_ixc = sem("token_table_copied")
        s_ovr = sem("overflow_table_ready")
        s_w1 = [sem(f"w1_loaded{s}") for s in range(RING)]
        s_w2 = [sem(f"w2_loaded{s}") for s in range(RING)]
        s_idn = sem("index_copied")
        s_xg = [sem(f"rows_gathered{s}") for s in range(XG)]
        s_xt = sem("rows_transposed")
        s_xtc = sem("rows_transpose_copied")
        s_gs = sem("gates_spread")
        s_gt = sem("gates_transposed")
        s_gtc = sem("gates_transpose_copied")
        s_gb = sem("gated_biases_done")
        s_g1 = sem("hidden_done")
        s_hnc = sem("hidden_copied")
        s_hT = sem("hidden_transposed")
        s_ha = sem("hidden_biased")
        s_hr = sem("hidden_ready")
        s_g2 = sem("result_done")
        s_yc = sem("result_copied")
        s_ys = [sem(f"result_stored{s}") for s in range(XG)]
        s_yo = sem("overflow_result_stored")
        s_all = sem("all_results_stored")
        s_yg = [sem(f"token_results_loaded{h}") for h in range(2)]
        s_o = sem("output_ready")
        s_out = sem("output_stored")

        block = ctx.enter_context(nc.Block())

        MAIN_X0, MAIN_W0 = PAIRS // XG, PAIRS // RING
        over_slot = 0

        def gated_bias(t):
            bank, at = (ps[6 + t // 2], (t % 2) * D) if t < 4 else (ps[5], D)
            return bank[0:NP, at:at + D]

        PARTS_T = [(0, 2), (2, NT)]

        def load_results(eng, k, h, a, b):
            rows = y_dram[1 + k * NODES:1 + (k + 1) * NODES, :].rearrange("(p t) d -> p t d", t=NT)
            eng.dma_start(yg[:, k, a:b, :], rows[:, a:b, :]).then_inc(s_yg[h], 16)

        @block.sync
        def _(sp):
            sp.dma_start(e_dst[:, :], dst.rearrange("(g e) -> g e", g=GROUPS)).then_inc(s_ed, 16)
            sp.dma_start(e_src[:, :], src.rearrange("(g e) -> g e", g=GROUPS)).then_inc(s_ed, 16)
            sp.dma_start(e_f[:, 2, :], ew.rearrange("(g e) -> g e", g=GROUPS)).then_inc(s_ed, 16)
            sp.dma_start(xs[:, :, :], x.rearrange("(p t) d -> p t d", t=NT)).then_inc(s_x, 16)
            sp.dma_start(epsb[:, :], eps.rearrange("(a b) -> a b", a=1).to_broadcast([128, 1])).then_inc(s_eps, 16)
            sp.dma_start(w1g[:, :, :], W1.rearrange("(k p) f -> p k f", k=2)).then_inc(s_par, 16)
            for n, v in enumerate((b1, g1, be1, b2, g2, be2)):
                sp.dma_start(vec[2 * n:2 * n + 2, :], v.rearrange("(o p) -> o p", o=2)).then_inc(s_vec, 16)
            sp.dma_start(w2g[:, :, :], W2.rearrange("(k p) f -> p k f", k=2)).then_inc(s_par, 16)
            sp.dma_start(wrs[:, :, :], Wr.rearrange("(k p) f -> p k f", k=2)).then_inc(s_rt, 16)
            sp.dma_start(brs[:, :], br.rearrange("(a n) -> a n", a=1)).then_inc(s_rt, 16)
            sp.dma_start(fb1s[:, :], fb1).then_inc(s_fb, 16)
            sp.dma_start(fb2s[:, :], fb2).then_inc(s_fb, 16)

            f1 = F1.rearrange("e (p k) f -> p e (k f)", k=2)
            f2 = F2.rearrange("e (p j) f -> p e (j f)", j=4)
            for s in range(RING):
                sp.dma_start(w1r[:, s, :, :], f1[:, 2 * s:2 * s + 2, :]).then_inc(s_w1[s], 16)
                sp.dma_start(w2r[:, s, :, :], f2[:, 2 * s:2 * s + 2, :]).then_inc(s_w2[s], 16)
            with sp.Fori(1, PAIRS // RING) as i:
                for s in range(RING):
                    c = i * RING + s
                    sp.wait_ge(s_g1, c - RING + 1)
                    sp.dma_start(w1r[:, s, :, :], f1[:, bass.ds(c * 2, 2), :]).then_inc(s_w1[s], 16)
                    sp.wait_ge(s_g2, c - RING + 1)
                    sp.dma_start(w2r[:, s, :, :], f2[:, bass.ds(c * 2, 2), :]).then_inc(s_w2[s], 16)

            sp.wait_ge(s_ovr, 1)
            any_over = sp.value_load(oflag[0:1, 0:1], min_val=0, max_val=1)
            with sp.If(any_over):
                with sp.Fori(0, OVER_PAIRS) as j:
                    used = sp.value_load(oflag[0:1, bass.ds(j, 1)], min_val=0, max_val=1)
                    with sp.If(used):
                        sp.wait_ge(s_g1, j + PAIRS)
                        sp.wait_ge(s_g2, j + PAIRS)
                        for half in range(2):
                            e = sp.value_load(oexp[0:1, bass.ds(j * 2 + half, 1)], min_val=0, max_val=EXPERTS - 1)
                            sp.dma_start(w1r[:, over_slot, half, :], f1[:, bass.ds(e, 1), :].rearrange("p a f -> p (a f)")).then_inc(s_w1[over_slot], 16)
                            sp.dma_start(w2r[:, over_slot, half, :], f2[:, bass.ds(e, 1), :].rearrange("p a f -> p (a f)")).then_inc(s_w2[over_slot], 16)
                        sp.nop()
                sp.nop()

            sp.wait_ge(s_all, 1)
            for h, (a, b) in enumerate(PARTS_T):
                load_results(sp, 0, h, a, b)
            sp.wait_ge(s_o, 1)
            sp.dma_start(out.rearrange("(p t) d -> p t d", t=NT)[:, 0:PARTS_T[0][1], :], os[:, 0:PARTS_T[0][1], :]).then_inc(s_out, 16)
            sp.wait_ge(s_out, 32)

        @block.gpsimd
        def _(pool):
            steps = [0]

            def link(ins):
                steps[0] += 1
                ins.then_inc(s_pool, 1)
                pool.wait_ge(s_pool, steps[0])

            pool.iota(iota_src[:, :, :], pattern=[[1, NT], [NT, 128]], base=0, channel_multiplier=0,
                      allow_small_or_imprecise_dtypes=True)
            pool.iota(iota_c[:, :], pattern=[[1, 128]], base=0, channel_multiplier=0,
                      allow_small_or_imprecise_dtypes=True).then_inc(s_cst, 1)
            link(pool.memset(ident[:, :], 0.0))
            pool.affine_select(out=ident[:, :], in_=ident[:, :], compare_op=ALU.not_equal, fill=1.0, base=0,
                               pattern=[[-1, 128]], channel_multiplier=1).then_inc(s_cst, 1)
            pool.iota(w64[:, :, :], pattern=[[WIN, ROUNDS], [0, GROUPS]], base=0, channel_multiplier=0,
                      allow_small_or_imprecise_dtypes=True).then_inc(s_cst, 1)
            link(pool.memset(AT[:, :, :], 0.0))
            pool.affine_select(out=AT[:, :, :], in_=AT[:, :, :], compare_op=ALU.not_equal, fill=1.0, base=0,
                                    pattern=[[1, NT], [-1, AT_W]], channel_multiplier=NT).then_inc(s_at0, 1)
            pool.wait_ge(s_eps, 16)
            pool.tensor_scalar(epsb[:, :], epsb[:, :], 1.0, None, ALU.add).then_inc(s_cst, 1)

            def more_constants():
                link(pool.memset(tri[:, :], 1.0))
                pool.affine_select(out=tri[:, :], in_=tri[:, :], compare_op=ALU.is_gt, fill=0.0, base=0,
                                   pattern=[[1, NP]], channel_multiplier=-1)
                pool.memset(ones_b[:, :], 1.0)
                pool.memset(ones_r[:, :], 1.0)
                pool.iota(e64[:, :], pattern=[[CAP, EXPERTS]], base=0, channel_multiplier=0,
                          allow_small_or_imprecise_dtypes=True)
                pool.iota(tok[:, :], pattern=[[NODES, TOPK], [1, NT]], base=1, channel_multiplier=NT,
                          allow_small_or_imprecise_dtypes=True)
                pool.iota(spare[:, :], pattern=[[128, ALL_PAIRS]], base=ROWS, channel_multiplier=1,
                          allow_small_or_imprecise_dtypes=True)
                pool.iota(bi[:, :], pattern=[[1, 2 * OVER_PAIRS]], base=0, channel_multiplier=0,
                          allow_small_or_imprecise_dtypes=True)
                pool.iota(pi2[:, :], pattern=[[2, OVER_PAIRS]], base=0, channel_multiplier=0,
                          allow_small_or_imprecise_dtypes=True).then_inc(s_cst, 1)

            more_constants()
            pool.wait_ge(s_ctl, 1)
            pool.wait_ge(s_at0, 2)

            def add_window(it, buf):
                pool.wait_ge(s_awc, it + 1)
                base = pool.value_load(bases[0:1, bass.ds(it, 1)], min_val=0, max_val=NODES - 1)
                win = AT[:, :, bass.ds(base, WIN)]
                pool.tensor_tensor(win, win, AWs[:, buf, :, :], ALU.add).then_inc(s_at, 1)

            add_window(0, 0)
            pool.wait_ge(s_at, 1)
            add_window(1, 1)
            with pool.Fori(1, GROUPS // 2) as i:
                for buf in range(2):
                    pool.wait_ge(s_at, i * 2 + buf)
                    add_window(i * 2 + buf, buf)
            any_more = pool.value_load(flags[0:1, 1:2], min_val=0, max_val=1)
            with pool.If(any_more):
                with pool.Fori(1, ROUNDS) as r:
                    more = pool.value_load(flags[0:1, bass.ds(r, 1)], min_val=0, max_val=1)
                    with pool.If(more):
                        with pool.Fori(0, GROUPS // 2) as i:
                            for buf in range(2):
                                it = r * GROUPS + i * 2 + buf
                                pool.wait_ge(s_at, it)
                                add_window(it, buf)
                        pool.nop()
                pool.nop()

            def copy_index(c, s):
                pool.tensor_copy(idn[:, s, :], idx[:, bass.ds(c, 1), :].rearrange("p a b -> p (a b)")).then_inc(s_idn, 1)

            def gather(s, xslot):
                pool.indirect_dma_start(out=xg[:, xslot, :], out_offset=None, in_=xf_dram,
                                        in_offset=bass.IndirectOffsetOnAxis(ap=idn[:, s, 0:1], axis=0),
                                        bounds_check=ROWS - 1).then_inc(s_xg[xslot], 16)

            def scatter(s, stored):
                pool.indirect_dma_start(out=y_dram, out_offset=bass.IndirectOffsetOnAxis(ap=idn[:, s, 1:2], axis=0),
                                        in_=ys[:, s % XG, :], in_offset=None,
                                        bounds_check=ROWS + ALL_PAIRS * 128 - 1).then_inc(stored, 16)

            def step(c, s, turn):
                static = isinstance(c, int)
                if not static or c >= XG:
                    pool.wait_ge(s_xt, c - XG + 1)
                    pool.wait_ge(s_yc, c - XG + 1)
                if not static or c >= RING - 1:
                    pool.wait_ge(s_ys[(s + 1) % XG], turn * 16)
                pool.wait_ge(s_idn, c + 1)
                copy_index(c + 1, (s + 1) % RING)
                gather(s, s % XG)
                if not static or c >= XG:
                    scatter((s - XG) % RING, s_ys[s % XG])

            pool.wait_ge(s_ixc, 1)
            copy_index(0, 0)
            pool.wait_ge(s_xfd, 48)
            for c in range(RING):
                step(c, c, 1)
            with pool.Fori(1, PAIRS // RING) as i:
                for s in range(RING):
                    step(i * RING + s, s, i * (RING // XG) + (s + 1 - RING) // XG + 1)
            for c in range(PAIRS, PAIRS + XG):
                pool.wait_ge(s_yc, c - XG + 1)
                scatter((c - XG) % RING, s_ys[c % XG])
            for s in range(XG):
                pool.wait_ge(s_ys[s], 16 * MAIN_X0)
            pool.wait_ge(s_idn, PAIRS + 1)
            pool.wait_ge(s_ovr, 1)
            any_over = pool.value_load(oflag[0:1, 0:1], min_val=0, max_val=1)
            with pool.If(any_over):
                with pool.Fori(0, OVER_PAIRS) as j:
                    used = pool.value_load(oflag[0:1, bass.ds(j, 1)], min_val=0, max_val=1)
                    with pool.If(used):
                        pool.wait_ge(s_xt, j + PAIRS)
                        copy_index(j + PAIRS, over_slot)
                        pool.wait_ge(s_idn, j + PAIRS + 2)
                    with pool.If(used):
                        gather(over_slot, over_slot)
                        pool.wait_ge(s_yc, j + PAIRS + 1)
                    with pool.If(used):
                        scatter(over_slot, s_yo)
                        pool.wait_ge(s_yo, (j + 1) * 16)
                        pool.nop()
                pool.nop()
            pool.memset(done[:, :], 0.0).then_inc(s_all, 1)

        @block.scalar
        def _(act):
            act.wait_ge(s_var, 1)
            act.activation(nrm[0:NP, 1, :], nrm[0:NP, 0, :], ACT.Sqrt).then_inc(s_std, 1)
            act.wait_ge(s_cst, 4)
            act.wait_ge(s_at0, 1)
            act.activation(AT[:, :, :], AT[:, :, :], ACT.Copy, scale=epsb[:, 0:1]).then_inc(s_at0, 1)
            act.wait_ge(s_vt, 1)
            act.activation(vecT[:, :], ps[7][:, 0:NVEC], ACT.Copy).then_inc(s_vc, 1)
            for t in range(NT):
                act.wait_ge(s_nt, t + 1)
                act.activation(nT[:, :, t * NP:(t + 1) * NP],
                               ps[2 + t % 2][:, 0:2 * NP].rearrange("p (k n) -> p k n", k=2), ACT.Copy).then_inc(s_ntc, 1)
            for t in range(NT):
                act.wait_ge(s_xw, t + 1)
                act.activation(xw[:, t, :], ps[4 + t % 2][0:NP, 0:D], ACT.Copy).then_inc(s_xwc, 1)
            act.wait_ge(s_ctl, 1)

            def copy_window(it, buf):
                act.wait_ge(s_aw, it + 1)
                act.activation(AWs[:, buf, :, :], ps[buf][:, 0:NT * WIN].rearrange("p (s w) -> p s w", s=NT),
                               ACT.Copy).then_inc(s_awc, 1)

            copy_window(0, 0)
            copy_window(1, 1)
            with act.Fori(1, GROUPS // 2) as i:
                for buf in range(2):
                    act.wait_ge(s_at, i * 2 + buf - 1)
                    copy_window(i * 2 + buf, buf)
            any_more = act.value_load(flags[0:1, 1:2], min_val=0, max_val=1)
            with act.If(any_more):
                with act.Fori(1, ROUNDS) as r:
                    more = act.value_load(flags[0:1, bass.ds(r, 1)], min_val=0, max_val=1)
                    with act.If(more):
                        with act.Fori(0, GROUPS // 2) as i:
                            for buf in range(2):
                                it = r * GROUPS + i * 2 + buf
                                act.wait_ge(s_at, it - 1)
                                copy_window(it, buf)
                        act.nop()
                act.nop()

            for layer in range(2):
                bank0 = 4 - 4 * layer
                for o in range(2):
                    for c, (a, b) in enumerate(CHUNKS):
                        act.wait_ge(s_h, 4 * layer + 2 * o + c + 1)
                        act.activation(hT[:, o, a:b], ps[bank0 + 2 * o + c][:, 0:b - a], ACT.Identity,
                                       bias=vecT[:, 6 * layer + o:6 * layer + o + 1]).then_inc(s_hc, 1)
                    act.wait_ge(s_var, 2 + 2 * layer + o)
                    act.activation(nrm[:, 1, o:o + 1], nrm[:, 0, o:o + 1], ACT.Sqrt).then_inc(s_std, 1)
                act.wait_ge(s_bn, 2 * layer + 2)
                act.activation((nT, hT)[layer][:, 1, :], hT[:, 1, :], ACT.Identity, bias=nrm[:, 5, 1:2],
                               scale=nrm[:, 4, 1:2]).then_inc(s_hn, 1)
            act.wait_ge(s_var, 6)
            act.activation(nrm[0:NP, 1, :], nrm[0:NP, 0, :], ACT.Sqrt).then_inc(s_std, 1)
            act.wait_ge(s_xn, 2 * NT)
            for k in range(TOPK):
                act.dma_start(xf_dram[1 + k * NODES:1 + (k + 1) * NODES, :].rearrange("(p t) d -> p (t d)", t=NT),
                              xn[:, :, :].rearrange("p t d -> p (t d)")).then_inc(s_xfd, 16)
            act.dma_start(xf_dram[0:1, :], xn[0:1, 0, :]).then_inc(s_xfd, 16)
            for t in range(NT):
                act.wait_ge(s_nt, NT + t + 1)
                act.activation(nT[:, :, t * NP:(t + 1) * NP],
                               ps[t % 2][:, 0:2 * NP].rearrange("p (k n) -> p k n", k=2), ACT.Copy).then_inc(s_ntc, 1)
            act.wait_ge(s_lg, 1)
            act.activation(lg[:, :, :], ps[3][0:NP, 0:NT * EXPERTS].rearrange("p (t e) -> p t e", t=NT), ACT.Copy).then_inc(s_lgc, 1)
            act.wait_ge(s_ld, 1)
            act.activation(gt[:, 1, :], gt[:, 0, :], ACT.Exp).then_inc(s_le, 1)

            act.wait_ge(s_bi, 1)
            act.activation(b1T[:, :, :], ps[6][:, 0:4 * EXPERTS].rearrange("p (j e) -> p j e", j=4), ACT.Copy).then_inc(s_bic, 1)
            act.wait_ge(s_gt, 1)
            act.activation(GT[:, 0:4 * NP], ps[3][0:EXPERTS, 0:4 * NP], ACT.Copy)
            act.activation(GT[:, 4 * NP:NODES], ps[5][0:EXPERTS, 0:NP], ACT.Copy).then_inc(s_gtc, 1)

            def copy_rows(c, par):
                act.wait_ge(s_xt, c + 1)
                act.activation(xgT[:, par, :, :], ps[par][:, 0:256].rearrange("p (k n) -> p k n", k=2),
                               ACT.Copy).then_inc(s_xtc, 1)

            def relu(c, par):
                act.wait_ge(s_ha, c + 1)
                act.activation(hr[:, par, :, :], hb[:, :, :], ACT.Relu).then_inc(s_hr, 1)

            def step(c, s):
                static = isinstance(c, int)
                if not static or c >= 2:
                    act.wait_ge(s_g1, c - 1)
                copy_rows(c, s % 2)
                if not static or c >= 1:
                    if not static or c >= 3:
                        act.wait_ge(s_g2, c - 2)
                    relu(c - 1, (s - 1) % 2)

            for c in range(RING):
                step(c, c)
            with act.Fori(1, PAIRS // RING) as i:
                for s in range(RING):
                    step(i * RING + s, s)
            act.wait_ge(s_g2, PAIRS - 2)
            relu(PAIRS - 1, (PAIRS - 1) % 2)

            act.wait_ge(s_ovr, 1)
            any_over = act.value_load(oflag[0:1, 0:1], min_val=0, max_val=1)
            with act.If(any_over):
                with act.Fori(0, OVER_PAIRS) as j:
                    used = act.value_load(oflag[0:1, bass.ds(j, 1)], min_val=0, max_val=1)
                    with act.If(used):
                        c = j + PAIRS
                        act.wait_ge(s_yc, c)
                        copy_rows(c, 0)
                        relu(c, 0)
                        act.nop()
                act.nop()
            act.wait_ge(s_all, 1)
            for h, (a, b) in enumerate(PARTS_T):
                load_results(act, 1, h, a, b)
            act.wait_ge(s_o, 2)
            act.dma_start(out.rearrange("(p t) d -> p t d", t=NT)[:, PARTS_T[1][0]:NT, :], os[:, PARTS_T[1][0]:NT, :]).then_inc(s_out, 16)

        @block.vector
        def _(dve):
            steps = [0]

            def link(ins):
                steps[0] += 1
                ins.then_inc(s_dve, 1)
                dve.wait_ge(s_dve, steps[0])

            def rsqrt(p, n, count):
                v, sd, r, t = (nrm[0:p, k, n] for k in range(4))
                dve.wait_ge(s_std, count)
                link(dve.reciprocal(r, sd))
                link(dve.tensor_tensor(t, r, r, ALU.mult))
                link(dve.scalar_tensor_tensor(out=t, in0=t, scalar=-0.5, in1=v, op0=ALU.mult, op1=ALU.mult))
                link(dve.scalar_tensor_tensor(out=r, in0=t, scalar=1.5, in1=r, op0=ALU.add, op1=ALU.mult))

            dve.wait_ge(s_ed, 48)
            dve.tensor_copy(e_f[:, 0, :], e_src[:, :])
            link(dve.tensor_copy(e_f[:, 1, :], e_dst[:, :]))
            dve.tensor_reduce(dlo[:, 1:2], e_f[:, 1, :], AX.X, ALU.max)
            link(dve.tensor_reduce(dlo[:, 0:1], e_f[:, 1, :], AX.X, ALU.min))
            dve.tensor_tensor(dlo[:, 2:3], dlo[:, 1:2], dlo[:, 0:1], ALU.subtract)
            dve.tensor_scalar(e_f[:, 1, :], e_f[:, 1, :], dlo[:, 0:1], None, ALU.subtract).then_inc(s_ef, 1)
            dve.wait_ge(s_x, 16)
            for t in range(NT):
                ins = dve.bn_stats(st[0:NP, t, :], xs[:, t, :])
            link(ins)
            for t in range(NT):
                ins = dve.bn_aggr(mv[0:NP, t, :], st[0:NP, t, :])
            link(ins)
            dve.tensor_scalar(nrm[0:NP, 0, :], mv[0:NP, :, 1], EPS, None, ALU.add).then_inc(s_var, 1)
            dve.wait_ge(s_et, 1)
            et = ps[6][0:EP, 0:3 * QUADS * GROUPS].rearrange("p (c g) -> p g c", g=GROUPS)
            link(dve.tensor_copy(EF[:, :, 0:3 * QUADS], et))
            w = [EF[:, :, (2 + k) * QUADS:(3 + k) * QUADS] for k in range(PARTS)]
            wbv = wb[:, :].rearrange("p (g q) -> p g q", g=GROUPS)
            for k in range(1, PARTS):
                link(dve.tensor_copy(wbv, w[k - 1]))
                link(dve.tensor_tensor(w[k], w[k - 1], wbv, ALU.subtract))
            link(dve.tensor_copy(drow[:, :], ps[7][0:1, 64:64 + 2 * GROUPS]))
            link(dve.tensor_reduce(span[:, :], drow[0:1, GROUPS:2 * GROUPS], AX.X, ALU.max))
            dve.wait_ge(s_cst, 3)
            dve.tensor_scalar(flags[:, :], w64[:, :, 0], span[0:1, 0:1], None, ALU.is_le)
            link(dve.tensor_tensor(bases_f[:, :, :], w64[:, :, :],
                                   drow[0:1, 0:GROUPS].unsqueeze(1).to_broadcast([1, ROUNDS, GROUPS]), ALU.add))
            dve.tensor_scalar(bases[:, :], bases_f[:, :, :].rearrange("p r g -> p (r g)"), float(NODES - 1), None,
                              ALU.min).then_inc(s_ctl, 1)
            rsqrt(NP, slice(0, NT), 1)
            for t in range(NT):
                dve.tensor_scalar(xn[:, t, :], xs[:, t, :], mv[0:NP, t, 0:1], nrm[0:NP, 2, t:t + 1],
                                  ALU.subtract, ALU.mult).then_inc(s_xn, 1)
            dve.wait_ge(s_ctl, 1)

            def onehots(buf):
                parts = EFs[:, (buf * 5 + 2) * QUADS:(buf + 1) * 5 * QUADS].rearrange("p (k q) -> p k q", k=PARTS)
                for q in range(QUADS):
                    f = [EFs[:, buf * 5 * QUADS + k * QUADS + q:buf * 5 * QUADS + k * QUADS + q + 1] for k in range(5)]
                    dve.tensor_scalar(S[:, buf, q, :], iota_src[0:EP, :, :].rearrange("p t n -> p (t n)"), f[0], None, ALU.is_equal)
                    ins = dve.scalar_tensor_tensor(
                        out=Dw[:, buf, q, :, :], in0=iota_c[0:EP, 0:WIN].unsqueeze(1).to_broadcast([EP, PARTS, WIN]),
                        scalar=f[1], in1=parts[:, :, q:q + 1].to_broadcast([EP, PARTS, WIN]),
                        op0=ALU.is_equal, op1=ALU.mult)
                ins.then_inc(s_oh, 1)

            def two_groups(r, i):
                for buf in range(2):
                    it = r * GROUPS + i * 2 + buf
                    first = isinstance(it, int) and it < 2
                    fields = EFs[:, buf * 5 * QUADS:(buf + 1) * 5 * QUADS]
                    dve.wait_ge(s_ef, r + 1)
                    if not first:
                        dve.wait_ge(s_oh, it - 1)
                    dve.tensor_copy(fields, EF[:, bass.ds(i * 2 + buf, 1), :].rearrange("p g c -> p (g c)")).then_inc(s_efs, 1)
                    if not first:
                        dve.wait_ge(s_aw, it - 1)
                    dve.wait_ge(s_efs, it + 1)
                    onehots(buf)

            two_groups(0, 0)
            with dve.Fori(1, GROUPS // 2) as i:
                two_groups(0, i)
            any_more = dve.value_load(flags[0:1, 1:2], min_val=0, max_val=1)
            with dve.If(any_more):
                with dve.Fori(1, ROUNDS) as r:
                    more = dve.value_load(flags[0:1, bass.ds(r, 1)], min_val=0, max_val=1)
                    with dve.If(more):
                        dve.tensor_scalar(EF[:, :, QUADS:2 * QUADS], EF[:, :, QUADS:2 * QUADS], float(WIN), None,
                                          ALU.subtract).then_inc(s_ef, 1)
                        with dve.Fori(0, GROUPS // 2) as i:
                            two_groups(r, i)
                        dve.nop()
                dve.nop()

            for layer in range(2):
                for o in range(2):
                    for c, (a, b) in enumerate(CHUNKS):
                        dve.wait_ge(s_hc, 4 * layer + 2 * o + c + 1)
                        ins = dve.bn_stats(st[:, 2 * o + c, :], hT[:, o, a:b])
                    link(ins)
                    link(dve.bn_aggr(mv[:, o, :], st[:, 2 * o:2 * o + 2, :]))
                    dve.tensor_scalar(nrm[:, 0, o:o + 1], mv[:, o, 1:2], EPS, None, ALU.add).then_inc(s_var, 1)
                    rsqrt(128, slice(o, o + 1), 2 + 2 * layer + o)
                    if layer == 0 and o == 0:
                        dve.wait_ge(s_vc, 1)
                    gain, shift = (vecT[:, 6 * layer + 2 * k + o:6 * layer + 2 * k + o + 1] for k in (1, 2))
                    link(dve.tensor_tensor(nrm[:, 4, o:o + 1], nrm[:, 2, o:o + 1], gain, ALU.mult))
                    link(dve.tensor_tensor(nrm[:, 3, o:o + 1], nrm[:, 4, o:o + 1], mv[:, o, 0:1], ALU.mult))
                    dve.tensor_tensor(nrm[:, 5, o:o + 1], shift, nrm[:, 3, o:o + 1], ALU.subtract).then_inc(s_bn, 1)
                    if o == 0:
                        dve.wait_ge(s_bn, 2 * layer + 1)
                        dve.tensor_scalar((nT, hT)[layer][:, 0, :], hT[:, 0, :], nrm[:, 4, 0:1], nrm[:, 5, 0:1],
                                          ALU.mult, ALU.add).then_inc(s_hn, 1)
            for t in range(NT):
                dve.wait_ge(s_bt, t + 1)
                dve.tensor_tensor(x1[:, t, :], ps[4 + t % 4][0:NP, 0:D], xs[:, t, :], ALU.add).then_inc(s_x1, 1)
                dve.wait_ge(s_x1, t + 1)
                ins = dve.bn_stats(st[0:NP, t, :], x1[:, t, :])
            link(ins)
            for t in range(NT):
                ins = dve.bn_aggr(mv[0:NP, t, :], st[0:NP, t, :])
            link(ins)
            dve.tensor_scalar(nrm[0:NP, 0, :], mv[0:NP, :, 1], EPS, None, ALU.add).then_inc(s_var, 1)
            rsqrt(NP, slice(0, NT), 6)
            for t in range(NT):
                dve.tensor_scalar(xn[:, t, :], x1[:, t, :], mv[0:NP, t, 0:1], nrm[0:NP, 2, t:t + 1],
                                  ALU.subtract, ALU.mult).then_inc(s_xn, 1)

            dve.wait_ge(s_lgc, 1)
            for t in range(NT):
                ins = dve.max(m8[:, t, :], lg[:, t, :])
            link(ins)
            for t in range(NT):
                ins = dve.max_index(i8[:, t, :], m8[:, t, :], lg[:, t, :])
            dve.tensor_tensor(gt[:, 0, :], m8[:, :, 1], m8[:, :, 0], ALU.subtract).then_inc(s_ld, 1)
            dve.wait_ge(s_ld, 1)
            link(dve.tensor_copy(ixf[:, :, :], i8[:, :, 0:TOPK].rearrange("p t k -> p k t")))
            dve.wait_ge(s_cst, 5)
            experts = iota_c[0:NP, 0:EXPERTS].unsqueeze(1).to_broadcast([NP, TOPK * NT, EXPERTS])
            link(dve.tensor_tensor(Sel[:, :, :, :].rearrange("p k t e -> p (k t) e"), experts,
                                   ixf[:, :, :].rearrange("p k t -> p (k t)").unsqueeze(2).to_broadcast([NP, TOPK * NT, EXPERTS]),
                                   ALU.is_equal))
            dve.tensor_tensor(Mb[:, :, :], Sel[:, 0, :, :], Sel[:, 1, :, :], ALU.add).then_inc(s_m, 1)
            dve.wait_ge(s_rk, 1)
            link(dve.tensor_scalar(cnt_i[:, :], ps[4][0:NP, 0:EXPERTS], float(CAP - 1), None, ALU.add))
            link(dve.tensor_scalar(blk_i[:, :], cnt_i[:, :], 6, None, ALU.arith_shift_right))
            link(dve.tensor_scalar(ov[:, :], blk_i[:, :], 1.0, 0.0, ALU.subtract, ALU.max))
            link(dve.memset(cnt[:, :], 0.0))
            link(dve.tensor_tensor_scan(cum[:, :], ov[:, :], cnt[:, :], 0.0, ALU.add, ALU.add))
            link(dve.tensor_tensor(dlt[:, :], cum[:, :], ov[:, :], ALU.subtract))
            link(dve.tensor_scalar(dlt[:, :], dlt[:, :], float(CAP), float((EXPERTS - 1) * CAP), ALU.mult, ALU.add))
            link(dve.tensor_tensor(dlt[:, :], dlt[:, :], e64[:, :], ALU.subtract))
            rank = ps[7][0:NP, 0:NT * EXPERTS].rearrange("p (t e) -> p t e", t=NT)

            def over_tiles(a):
                return a.unsqueeze(1).to_broadcast([NP, NT, EXPERTS])

            link(dve.scalar_tensor_tensor(out=slm[:, :, :], in0=rank, scalar=float(CAP), in1=over_tiles(dlt[:, :]),
                                          op0=ALU.is_ge, op1=ALU.mult))
            link(dve.tensor_tensor(slm[:, :, :], slm[:, :, :], over_tiles(e64[:, :]), ALU.add))
            link(dve.tensor_tensor(slm[:, :, :], slm[:, :, :], rank, ALU.add))
            for k in range(TOPK):
                ins = dve.tensor_tensor(sly[:, k, :, :], slm[:, :, :], Sel[:, k, :, :], ALU.mult)
            link(ins)
            link(dve.tensor_reduce(slf[:, :], sly[:, :, :, :].rearrange("p k t e -> p (k t) e"), AX.X, ALU.add))
            link(dve.tensor_copy(sli[:, :], slf[:, :]))
            dve.tensor_scalar(lohi[:, 0, :], sli[:, :], 127, None, ALU.bitwise_and)
            link(dve.tensor_scalar(lohi[:, 1, :], sli[:, :], 7, None, ALU.logical_shift_right))
            link(dve.tensor_copy(lhf[:, :, :], lohi[:, :, :]))
            for m in range(TOPK * NT):
                dve.tensor_scalar(LO[:, m, :], iota_c[0:NP, :], lhf[:, 0, m:m + 1], None, ALU.is_equal)
                dve.tensor_scalar(HI[:, m, :], iota_c[0:NP, 0:ALL_PAIRS], lhf[:, 1, m:m + 1],
                                  tok[:, m:m + 1], ALU.is_equal, ALU.mult).then_inc(s_lh, 1)
            dve.wait_ge(s_ix, 1)
            rows = ps[5][:, 0:ALL_PAIRS]
            link(dve.scalar_tensor_tensor(out=dsf[:, :], in0=rows, scalar=0.0, in1=spare[:, :],
                                          op0=ALU.is_equal, op1=ALU.mult))
            dve.tensor_copy(idx[:, :, 0], rows)
            dve.tensor_tensor(idx[:, :, 1], dsf[:, :], rows, ALU.add).then_inc(s_ixc, 1)
            dve.tensor_scalar(oflag[:, :], pi2[:, :], cum[0:1, EXPERTS - 1:EXPERTS], None, ALU.is_lt)
            link(dve.tensor_tensor(ocmp[:, :, :], bi[0:1, :].unsqueeze(2).to_broadcast([1, 2 * OVER_PAIRS, EXPERTS]),
                                   cum[0:1, :].unsqueeze(1).to_broadcast([1, 2 * OVER_PAIRS, EXPERTS]), ALU.is_ge))
            link(dve.tensor_reduce(oexp_f[:, :], ocmp[:, :, :], AX.X, ALU.add))
            dve.tensor_scalar(oexp[:, :], oexp_f[:, :], float(EXPERTS - 1), None, ALU.min).then_inc(s_ovr, 1)
            dve.wait_ge(s_le, 1)
            link(dve.tensor_scalar(gt[:, 2, :], gt[:, 1, :], 1.0, None, ALU.add))
            link(dve.reciprocal(gt[:, 3, :], gt[:, 2, :]))
            link(dve.tensor_tensor(gt[:, 4, :], gt[:, 1, :], gt[:, 3, :], ALU.mult))
            for k in range(TOPK):
                ins = dve.tensor_tensor(Sel[:, k, :, :], Sel[:, k, :, :],
                                        gt[:, 3 + k, :].unsqueeze(2).to_broadcast([NP, NT, EXPERTS]), ALU.mult)
            link(ins)
            dve.tensor_tensor(lg[:, :, :], Sel[:, 0, :, :], Sel[:, 1, :, :], ALU.add).then_inc(s_gs, 1)
            dve.wait_ge(s_gb, 1)
            for t in range(NT):
                dve.tensor_tensor(x1[:, t, :], x1[:, t, :], gated_bias(t), ALU.add).then_inc(s_x1, 1)
            dve.wait_ge(s_bic, 1)

            def bias_hidden(c, par, bias):
                dve.wait_ge(s_hT, c + 1)
                dve.tensor_tensor(hb[:, :, :].rearrange("p j (h n) -> p j h n", h=2),
                                  ps[4 + par][:, 0:512].rearrange("p (j h n) -> p j h n", j=4, h=2),
                                  bias.unsqueeze(3).to_broadcast([128, 4, 2, CAP]), ALU.add).then_inc(s_ha, 1)

            def copy_hidden(c, par):
                dve.wait_ge(s_g1, c + 1)
                dve.tensor_copy(hn[:, par, :], ps[2 + par][:, 0:HID]).then_inc(s_hnc, 1)

            def copy_result(c, par, slot):
                dve.wait_ge(s_g2, c + 1)
                dve.tensor_copy(ys[:, slot, :], ps[6 + par][:, 0:D]).then_inc(s_yc, 1)

            def step(c, s, turn):
                static = isinstance(c, int)
                if not static or c >= 1:
                    if not static or c >= 2:
                        dve.wait_ge(s_hr, c - 1)
                    bias_hidden(c - 1, (s - 1) % 2, b1T[:, :, bass.ds(c * 2 - 2, 2)])
                copy_hidden(c, s % 2)
                if not static or c >= 1:
                    if not static or c > XG:
                        dve.wait_ge(s_ys[(s - 1) % XG], turn * 16)
                    copy_result(c - 1, (s - 1) % 2, (s - 1) % XG)

            for c in range(RING):
                step(c, c, 1)
            with dve.Fori(1, PAIRS // RING) as i:
                for s in range(RING):
                    step(i * RING + s, s, i * (RING // XG) + (s - 1) // XG)
            last = PAIRS - 1
            dve.wait_ge(s_hr, last)
            bias_hidden(last, last % 2, b1T[:, :, 2 * last:2 * last + 2])
            dve.wait_ge(s_ys[last % XG], (MAIN_X0 - 1) * 16)
            copy_result(last, last % 2, last % XG)
            any_over = dve.value_load(oflag[0:1, 0:1], min_val=0, max_val=1)
            with dve.If(any_over):
                dve.wait_ge(s_ys[over_slot], MAIN_X0 * 16)
                with dve.Fori(0, OVER_PAIRS) as j:
                    used = dve.value_load(oflag[0:1, bass.ds(j, 1)], min_val=0, max_val=1)
                    with dve.If(used):
                        c = j + PAIRS
                        dve.wait_ge(s_ha, c)
                        for half in range(2):
                            e = dve.value_load(oexp[0:1, bass.ds(j * 2 + half, 1)], min_val=0, max_val=EXPERTS - 1)
                            ins = dve.tensor_copy(b1o[:, :, half:half + 1], b1T[:, :, bass.ds(e, 1)])
                        ins.then_inc(s_vc, 1)
                        copy_hidden(c, 0)
                        dve.wait_ge(s_vc, j + 2)
                        bias_hidden(c, 0, b1o[:, :, :])
                        copy_result(c, 0, over_slot)
                        dve.nop()
                dve.nop()
            for h, (a, b) in enumerate(PARTS_T):
                dve.wait_ge(s_yg[h], 32)
                for t in range(a, b):
                    ins = dve.scalar_tensor_tensor(out=acc[:, t, :], in0=yg[:, 0, t, :], scalar=gt[:, 3, t:t + 1],
                                                   in1=x1[:, t, :], op0=ALU.mult, op1=ALU.add)
                link(ins)
                for t in range(a, b):
                    ins = dve.scalar_tensor_tensor(out=os[:, t, :], in0=yg[:, 1, t, :], scalar=gt[:, 4, t:t + 1],
                                                   in1=acc[:, t, :], op0=ALU.mult, op1=ALU.add)
                ins.then_inc(s_o, 1)

        @block.tensor
        def _(pe):
            mm, idt = pe.matmul, ident
            pe.wait_ge(s_cst, 2)
            pe.wait_ge(s_ef, 1)
            for k, col in enumerate((0, 2)):
                pe.transpose(ps[7][0:1, 64 + k * GROUPS:64 + (k + 1) * GROUPS], dlo[:, col:col + 1], idt[0:GROUPS, 0:GROUPS])
            for f in range(3):
                for q in range(QUADS):
                    m = f * QUADS + q
                    ins = pe.transpose(ps[6][0:EP, m * GROUPS:(m + 1) * GROUPS], e_f[:, f, q * EP:(q + 1) * EP],
                                       idt[0:GROUPS, 0:GROUPS])
            ins.then_inc(s_et, 1)
            pe.wait_ge(s_ctl, 1)
            pe.wait_ge(s_vec, 96)
            pe.transpose(ps[7][:, 0:NVEC], vec[:, :], idt[0:NVEC, 0:NVEC]).then_inc(s_vt, 1)
            for t in range(NT):
                pe.wait_ge(s_xn, t + 1)
                if t >= 2:
                    pe.wait_ge(s_ntc, t - 1)
                for k in range(2):
                    ins = pe.transpose(ps[2 + t % 2][:, k * NP:(k + 1) * NP], xn[:, t, k * 128:(k + 1) * 128],
                                       idt[0:NP, 0:NP])
                ins.then_inc(s_nt, 1)
            pe.wait_ge(s_par, 32)
            for t in range(NT):
                pe.wait_ge(s_ntc, t + 1)
                if t >= 2:
                    pe.wait_ge(s_xwc, t - 1)
                for k in range(2):
                    ins = mm(ps[4 + t % 2][0:NP, 0:D], nT[:, k, t * NP:(t + 1) * NP], w1g[:, k, :],
                             start=(k == 0), stop=(k == 1))
                ins.then_inc(s_xw, 1)
            def group(it, buf):
                pe.wait_ge(s_oh, it + 1)
                for s in range(NT):
                    for q in range(QUADS):
                        for k in range(PARTS):
                            ins = mm(ps[buf][:, s * WIN:(s + 1) * WIN], S[:, buf, q, s * 128:(s + 1) * 128],
                                     Dw[:, buf, q, k, :], start=(q == 0 and k == 0),
                                     stop=(q == QUADS - 1 and k == PARTS - 1))
                ins.then_inc(s_aw, 1)

            group(0, 0)
            group(1, 1)
            with pe.Fori(1, GROUPS // 2) as i:
                for buf in range(2):
                    pe.wait_ge(s_awc, i * 2 + buf - 1)
                    group(i * 2 + buf, buf)
            any_more = pe.value_load(flags[0:1, 1:2], min_val=0, max_val=1)
            with pe.If(any_more):
                with pe.Fori(1, ROUNDS) as r:
                    more = pe.value_load(flags[0:1, bass.ds(r, 1)], min_val=0, max_val=1)
                    with pe.If(more):
                        with pe.Fori(0, GROUPS // 2) as i:
                            for buf in range(2):
                                it = r * GROUPS + i * 2 + buf
                                pe.wait_ge(s_awc, it - 1)
                                group(it, buf)
                        pe.wait_ge(s_at, (r + 1) * GROUPS)
                        pe.nop()
                pe.nop()

            pe.wait_ge(s_xwc, NT)
            pe.wait_ge(s_at, GROUPS)
            for o in range(2):
                for c, (a, b) in enumerate(CHUNKS):
                    for s in range(NT):
                        ins = mm(ps[4 + 2 * o + c][:, 0:b - a], xw[:, s, o * 128:(o + 1) * 128], AT[0:NP, s, a:b],
                                 start=(s == 0), stop=(s == NT - 1))
                    ins.then_inc(s_h, 1)
            pe.wait_ge(s_hn, 2)
            for o in range(2):
                for c, (a, b) in enumerate(CHUNKS):
                    for k in range(2):
                        ins = mm(ps[2 * o + c][:, 0:b - a], w2g[:, k, o * 128:(o + 1) * 128], nT[:, k, a:b],
                                 start=(k == 0), stop=(k == 1))
                    ins.then_inc(s_h, 1)
            pe.wait_ge(s_hn, 4)
            for t in range(NT):
                if t >= 4:
                    pe.wait_ge(s_x1, t - 3)
                for k in range(2):
                    ins = pe.transpose(ps[4 + t % 4][0:NP, k * 128:(k + 1) * 128], hT[:, k, t:NODES:NT], idt[:, :])
                ins.then_inc(s_bt, 1)
            for t in range(NT):
                pe.wait_ge(s_xn, NT + t + 1)
                if t >= 2:
                    pe.wait_ge(s_ntc, NT + t - 1)
                for k in range(2):
                    ins = pe.transpose(ps[t % 2][:, k * NP:(k + 1) * NP], xn[:, t, k * 128:(k + 1) * 128],
                                       idt[0:NP, 0:NP])
                ins.then_inc(s_nt, 1)
            pe.wait_ge(s_rt, 32)
            pe.wait_ge(s_cst, 5)
            for t in range(NT):
                pe.wait_ge(s_ntc, NT + t + 1)
                lgp = ps[3][0:NP, t * EXPERTS:(t + 1) * EXPERTS]
                for k in range(2):
                    mm(lgp, nT[:, k, t * NP:(t + 1) * NP], wrs[:, k, :], start=(k == 0), stop=False)
                ins = mm(lgp, ones_r[:, :], brs[:, :], start=False, stop=True)
            ins.then_inc(s_lg, 1)
            pe.wait_ge(s_fb, 32)
            for j in range(4):
                ins = pe.transpose(ps[6][:, j * EXPERTS:(j + 1) * EXPERTS], fb1s[:, j:HID:4], idt[0:EXPERTS, 0:EXPERTS])
            ins.then_inc(s_bi, 1)
            pe.wait_ge(s_m, 1)
            for t in range(NT):
                for u in range(t + 1):
                    mm(ps[7][0:NP, t * EXPERTS:(t + 1) * EXPERTS], ones_b[:, :] if u < t else tri[:, :], Mb[:, u, :],
                       start=(u == 0), stop=(u == t))
            for u in range(NT):
                ins = mm(ps[4][0:NP, 0:EXPERTS], ones_b[:, :], Mb[:, u, :], start=(u == 0), stop=(u == NT - 1))
            ins.then_inc(s_rk, 1)
            for m in range(TOPK * NT):
                pe.wait_ge(s_lh, m + 1)
                ins = mm(ps[5][:, 0:ALL_PAIRS], LO[:, m, :], HI[:, m, :], start=(m == 0), stop=(m == TOPK * NT - 1))
            ins.then_inc(s_ix, 1)

            pe.wait_ge(s_gs, 1)
            for t in range(NT):
                ins = pe.transpose(ps[3][0:EXPERTS, t * NP:(t + 1) * NP] if t < 4 else ps[5][0:EXPERTS, 0:NP],
                                   lg[:, t, :], idt[0:NP, 0:NP])
            ins.then_inc(s_gt, 1)
            pe.wait_ge(s_gtc, 1)
            pe.wait_ge(s_bic, 1)
            for t in range(NT):
                ins = mm(gated_bias(t), GT[:, t * NP:(t + 1) * NP], fb2s[:, :], start=True, stop=True)
            ins.then_inc(s_gb, 1)

            def rows_T(c, par, slot, gathered):
                pe.wait_ge(s_xg[slot], gathered)
                for k in range(2):
                    ins = pe.transpose(ps[par][:, k * 128:(k + 1) * 128], xg[:, slot, k:D:2], idt[:, :])
                ins.then_inc(s_xt, 1)

            def hidden(par, slot):
                for k in range(2):
                    for half in range(2):
                        rows = slice(half * CAP, (half + 1) * CAP)
                        ins = mm(ps[2 + par][rows, 0:HID], xgT[:, par, k, rows],
                                 w1r[:, slot, half, k * HID:(k + 1) * HID], start=(k == 0), stop=(k == 1))
                ins.then_inc(s_g1, 1)

            def hidden_T(c, par):
                pe.wait_ge(s_hnc, c + 1)
                for j in range(4):
                    ins = pe.transpose(ps[4 + par][:, j * 128:(j + 1) * 128], hn[:, par, j:HID:4], idt[:, :])
                ins.then_inc(s_hT, 1)

            def result(c, par, slot):
                pe.wait_ge(s_hr, c + 1)
                for j in range(4):
                    for half in range(2):
                        rows = slice(half * CAP, (half + 1) * CAP)
                        ins = mm(ps[6 + par][rows, 0:D], hr[:, par, j, rows],
                                 w2r[:, slot, half, j * D:(j + 1) * D], start=(j == 0), stop=(j == 3))
                ins.then_inc(s_g2, 1)

            def pair_result(c, s, loads):
                pe.wait_ge(s_w2[s], loads)
                if not isinstance(c, int) or c >= 2:
                    pe.wait_ge(s_yc, c - 1)
                result(c, s % 2, s)

            def step(c, s, gathered, loads, loads_before):
                static = isinstance(c, int)
                if not static or c >= 2:
                    pe.wait_ge(s_xtc, c - 1)
                rows_T(c, s % 2, s % XG, gathered)
                if not static or c >= 1:
                    hidden_T(c - 1, (s - 1) % 2)
                pe.wait_ge(s_w1[s], loads)
                pe.wait_ge(s_xtc, c + 1)
                hidden(s % 2, s)
                if not static or c >= 1:
                    if static and c == 1:
                        pe.wait_ge(s_x1, 2 * NT)
                    pair_result(c - 1, (s - 1) % RING, loads_before)

            for c in range(RING):
                step(c, c, 16 * (c // XG + 1), 16, 16)
            with pe.Fori(1, PAIRS // RING) as i:
                for s in range(RING):
                    step(i * RING + s, s, (i * (RING // XG) + s // XG + 1) * 16, (i + 1) * 16,
                         (i + 1) * 16 if s else i * 16)
            hidden_T(PAIRS - 1, (PAIRS - 1) % 2)
            pair_result(PAIRS - 1, RING - 1, 16 * MAIN_W0)
            pe.wait_ge(s_ovr, 1)
            any_over = pe.value_load(oflag[0:1, 0:1], min_val=0, max_val=1)
            with pe.If(any_over):
                with pe.Fori(0, OVER_PAIRS) as j:
                    used = pe.value_load(oflag[0:1, bass.ds(j, 1)], min_val=0, max_val=1)
                    with pe.If(used):
                        c = j + PAIRS
                        pe.wait_ge(s_yc, c)
                        rows_T(c, 0, over_slot, (j + MAIN_X0 + 1) * 16)
                        pe.wait_ge(s_w1[over_slot], (j * 2 + MAIN_W0 + 2) * 16)
                        pe.wait_ge(s_xtc, c + 1)
                        hidden(0, over_slot)
                        hidden_T(c, 0)
                        pe.wait_ge(s_w2[over_slot], (j * 2 + MAIN_W0 + 2) * 16)
                        result(c, 0, over_slot)
                        pe.nop()
                pe.nop()


_INS = ['x', 'src', 'dst', 'edge_weight', 'L0_gnn_W1', 'L0_gnn_b1', 'L0_gnn_g1', 'L0_gnn_be1', 'L0_gnn_W2',
        'L0_gnn_b2', 'L0_gnn_g2', 'L0_gnn_be2', 'L0_gnn_eps', 'L0_ffn_Wr', 'L0_ffn_br', 'L0_ffn_W1', 'L0_ffn_b1',
        'L0_ffn_W2', 'L0_ffn_b2']


def kernel(**inputs):
    import numpy as np
    import concourse.bacc as bacc
    from concourse import mybir
    from concourse.bass_utils import run_bass_kernel_spmd

    nc = bacc.Bacc("TRN2", target_bir_lowering=False, num_devices=1)
    arrays, args = {}, []
    for name in _INS:
        a = np.ascontiguousarray(inputs[name])
        arrays[f"in_{name}"] = a
        args.append(nc.dram_tensor(f"in_{name}", a.shape, mybir.dt.from_np(a.dtype), kind="ExternalInput").ap())
    args.append(nc.dram_tensor("out_0", (NODES, D), mybir.dt.float32, kind="ExternalOutput").ap())
    gnn_moe(nc, *args)
    r = run_bass_kernel_spmd(nc, [arrays], core_ids=[0])
    return r.results[0]["out_0"]
```

```python
import concourse.bass as bass
from concourse import mybir
from contextlib import ExitStack

FP32 = mybir.dt.float32
BF16 = mybir.dt.bfloat16
FP16 = mybir.dt.float16
I32 = mybir.dt.int32
U32 = mybir.dt.uint32
ALU = mybir.AluOpType
ACT = mybir.ActivationFunctionType
AX = mybir.AxisListType

NODES, EDGES, D, HID, EXPERTS, TOPK = 625, 10000, 256, 512, 64, 2
NT, NP = 5, 125
GROUPS, QUADS, EP = 20, 4, 125
GE = QUADS * EP
HEAD = 10
WIN = 40
ROUNDS = -(-NODES // WIN)
AT_W = NODES - 1 + WIN
PARTS = 3
CAP = 64
PAIRS = EXPERTS // 2
MAX_OVER = (NODES * TOPK - 2) // CAP
OVER_PAIRS = (MAX_OVER + 1) // 2
ALL_PAIRS = PAIRS + OVER_PAIRS
RING = 10
OWN = 8
FIRST = 12
AHEAD = 3
ROWS = 1 + TOPK * NODES
XG = 5
LAG = XG + 2
WARM = (7, 6, 22, 8, 12, 15)
EPS = 1e-5
C0 = 320
CHUNKS = [(0, C0), (C0, NODES)]
NVEC = 12


def gnn_moe(nc, x, src, dst, ew, W1, b1, g1, be1, W2, b2, g2, be2, eps, Wr, br, F1, fb1, F2, fb2, out):
    ctx = ExitStack()
    with ctx:
        def sb(name, shape, dt=FP32):
            return ctx.enter_context(nc.sbuf_tensor(name, shape, dt))

        def sem(name):
            return ctx.enter_context(nc.semaphore(name))

        def region(name, words, tensors):
            tile = sb(name, [128, words])

            def cut(*wanted):
                at, views = 0, []
                for shape, dt in wanted:
                    count = 1
                    for n in shape[1:]:
                        count *= n
                    size = -(-count * (2 if dt in (BF16, FP16) else 4) // 4)
                    assert at + size <= words, (name, at + size)
                    v = tile[0:shape[0], at:at + size]
                    if dt != FP32:
                        v = v.bitcast(dt)
                    letters = "abcd"[0:len(shape) - 1]
                    v = v.rearrange(f"p ({' '.join(letters)}) -> p {' '.join(letters)}",
                                    **dict(zip(letters, shape[1:])))
                    views.append(v)
                    at += size
                return views

            return [cut(*t) for t in tensors]

        xf_dram = nc.dram_tensor("xf_rows", [ROWS, D], FP32).ap()
        y_dram = nc.dram_tensor("y_rows", [ROWS + ALL_PAIRS * 128, D], FP32).ap()

        w1o = sb("w1_ring", [128, OWN, 2, 2 * HID])
        w2o = sb("w2_ring", [128, OWN, 2, 4 * D])
        ident = sb("ident", [128, 128])
        iota_c = sb("iota_c", [128, 128], FP16)
        tri = sb("tri", [NP, NP], BF16)
        ones_b = sb("ones_b", [NP, NP], BF16)
        e64b = sb("e64b", [1, NT, EXPERTS], BF16)
        e64s = sb("e64s", [1, EXPERTS])
        n64 = sb("n64", [NP, EXPERTS])
        tok = sb("tok", [NP, TOPK * NT])
        spare = sb("spare", [128, ALL_PAIRS])
        dsf = sb("dsf", [128, ALL_PAIRS])
        bi = sb("bi", [1, 2 * OVER_PAIRS])
        pi2 = sb("pi2", [1, OVER_PAIRS])
        xs = sb("xs", [NP, NT, D])
        wrs = sb("wrs", [128, 2, EXPERTS])
        brT = sb("brT", [128, 1])
        vec = sb("vec", [NVEC, 128])
        vecT = sb("vecT", [128, NVEC])
        epsb = sb("epsb", [128, 1])
        dlo = sb("dlo", [GROUPS, 4])
        drow = sb("drow", [1, 2 * GROUPS])
        span = sb("span", [1, 1])
        flags = sb("flags", [1, ROUNDS], I32)
        EFs = sb("EFs", [EP, 2 * 5 * QUADS])
        st = sb("st", [128, NT, 6])
        mv = sb("mv", [128, NT, 2])
        nrm = sb("nrm", [128, 6, NT])
        bn_eps = sb("bn_eps", [128, 1])
        b1T = sb("b1T", [128, 4, EXPERTS])
        b1o = sb("b1o", [128, 4, 2])
        m8 = sb("m8", [NP, NT, 8])
        i8 = sb("i8", [NP, NT, 8], U32)
        ixf = sb("ixf", [NP, TOPK, NT])
        gt = sb("gt", [NP, 5, NT])
        Mb = sb("Mb", [NP, NT, EXPERTS], BF16)
        slf = sb("slf", [NP, TOPK * NT])
        sli = sb("sli", [NP, TOPK * NT], U32)
        lohi = sb("lohi", [NP, 2, TOPK * NT], U32)
        lhf = sb("lhf", [NP, 2, TOPK * NT])
        idx = sb("idx", [128, ALL_PAIRS], U32)
        ids = sb("ids", [128, ALL_PAIRS], U32)
        idn = sb("idn", [128, XG], U32)
        idm = sb("idm", [128, XG], U32)
        done = sb("done", [1, 1])
        cum = sb("cum", [NP, EXPERTS])
        oexp_f = sb("oexp_f", [1, 2 * OVER_PAIRS])
        oexp = sb("oexp", [1, 2 * OVER_PAIRS], I32)
        oflag = sb("oflag", [1, OVER_PAIRS], I32)
        (AT,), (w1_8, ys) = region("adjacency", max(NT * AT_W, 4 * HID + XG * D), [
            [([128, NT, AT_W], FP32)],
            [([128, 2, 2 * HID], FP32), ([128, XG, D], FP32)]])
        (S,), (w1_9, xgT) = region("onehot_sources", 2 * QUADS * NT * 64, [
            [([EP, 2, QUADS, NT * 128], BF16)],
            [([128, 2, 2 * HID], FP32), ([128, 2, 2, 128], FP32)]])
        (AWs, Dw, dhot), (lgT, G1), (ocmp,) = region("windows", 2 * OVER_PAIRS * EXPERTS, [
            [([128, 2, NT, WIN], FP32), ([EP, 2, QUADS, PARTS, WIN], BF16),
             ([EP, 2, QUADS, WIN], BF16)],
            [([128, 3 * NP], FP32), ([NP, NT, EXPERTS], FP32)],
            [([1, 2 * OVER_PAIRS, EXPERTS], FP32)]])
        (iota_src, w64, bases), (GT,) = region("windows_and_nodes", NT * 64 + 2 * ROUNDS * GROUPS, [
            [([128, NT, 128], FP16), ([1, ROUNDS, GROUPS], FP32), ([1, ROUNDS * GROUPS], I32)],
            [([EXPERTS, NODES], FP32)]])
        (w1g, w2g, fb1s, EF, wb, sabs), (w2_8,) = region("gnn_parameters", 4 * D + HID + GROUPS * QUADS * 5 + GROUPS * 2 + NT * 64, [
            [([128, 2, D], FP32), ([128, 2, D], FP32), ([EXPERTS, HID], FP32), ([EP, GROUPS, 5 * QUADS], FP32),
             ([EP, GROUPS * QUADS], BF16), ([EP, NT * 128], FP16)],
            [([128, 2, 4 * D], FP32)]])
        (e_src, e_dst, e_f), (Sel, lg, slm, LO, HI), (hr, hn) = region("edge_rows", 5 * GE, [
            [([GROUPS, GE], I32), ([GROUPS, GE], I32), ([GROUPS, 3, GE], FP32)],
            [([NP, TOPK, NT, EXPERTS], FP32), ([NP, NT, EXPERTS], FP32), ([NP, NT, EXPERTS], FP32),
             ([NP, TOPK * NT, 128], FP16), ([NP, TOPK * NT, ALL_PAIRS], FP16)],
            [([128, 2, 4, 128], FP32), ([128, 2, HID], FP32)]])
        (xn,), (hT,), (xg,) = region("xn_or_hT", NT * D, [
            [([NP, NT, D], FP32)], [([128, 2, NODES], FP32)], [([128, XG, D], FP32)]])
        (nT, xw), (sly, cnt_i, blk_i, ov, dlt), (w2_9, hb) = region("nT_xw", 2 * NODES + NT * D + 30, [
            [([128, 2, NODES], FP32), ([NP, NT, D], FP32)],
            [([NP, TOPK, NT, EXPERTS], FP32), ([NP, EXPERTS], I32), ([NP, EXPERTS], I32),
             ([NP, EXPERTS], FP32), ([NP, EXPERTS], FP32)],
            [([128, 2, 4 * D], FP32), ([128, 4, 128], FP32)]])
        fb2s = sb("fb2s", [EXPERTS, D])

        def w1r(slot):
            return w1o[:, slot, :, :] if slot < OWN else (w1_8, w1_9)[slot - OWN]

        def w2r(slot):
            return w2o[:, slot, :, :] if slot < OWN else (w2_8, w2_9)[slot - OWN]

        def uses(i, m, ring, back=0):
            return i * (RING // ring) + (m - back) // ring + 1

        x1 = xs
        yg = w1o[:, 0:2, :, :].rearrange("p a b c -> p (a b c)")[0:NP, 0:TOPK * NT * D].rearrange(
            "p (k t d) -> p k t d", k=TOPK, t=NT)
        os, acc = (w2o[:, s, :, :].rearrange("p a b -> p (a b)")[0:NP, 0:NT * D].rearrange("p (t d) -> p t d", t=NT)
                   for s in range(2))

        ps = [ctx.enter_context(nc.psum_tensor(f"bank{i}", [128, 512], FP32)) for i in range(8)]

        s_ed = sem("edges_loaded")
        s_x = sem("x_loaded")
        s_par = sem("gnn_weights_loaded")
        s_vec = sem("vectors_loaded")
        s_fb = sem("expert_biases_loaded")
        s_rt = sem("router_loaded")
        s_eps = sem("eps_loaded")
        s_pool = sem("pool_step")
        s_cst = sem("constants_made")
        s_at0 = sem("diagonal_made")
        s_dve = sem("dve_step")
        s_efs = sem("fields_copied")
        s_ef = sem("edge_fields_ready")
        s_et = sem("edge_fields_transposed")
        s_ctl = sem("rounds_ready")
        s_var = sem("variance_ready")
        s_std = sem("deviation_ready")
        s_xn = sem("normed_ready")
        s_lnf = sem("layer_norm_factors_ready")
        s_vt = sem("vectors_transposed")
        s_vc = sem("vectors_copied")
        s_nt = sem("normed_transposed")
        s_ntc = sem("normed_transpose_copied")
        s_xw = sem("xw_done")
        s_xwc = sem("xw_copied")
        s_oh = sem("onehots_ready")
        s_dh = sem("destination_onehots_ready")
        s_sa = sem("source_distance_ready")
        s_oha = sem("last_quad_sources_ready")
        s_aw = sem("window_done")
        s_awc = sem("window_copied")
        s_at = sem("window_added")
        s_h = sem("h_done")
        s_bn = sem("norm_factors_ready")
        s_hn = sem("h_normed_by_act")
        s_hd = sem("h_normed_by_dve")
        s_bt = sem("back_transposed")
        s_x1 = sem("x1_ready")
        s_bi = sem("expert_bias_transposed")
        s_bic = sem("expert_bias_copied")
        s_xfd = sem("xf_stored")
        s_lg = sem("logits_done")
        s_lgc = sem("logits_copied")
        s_lt = sem("logits_transposed")
        s_ld = sem("logit_gap_ready")
        s_le = sem("gap_exp_ready")
        s_m = sem("choice_mask_ready")
        s_rk = sem("ranks_done")
        s_lh = sem("slot_onehots_ready")
        s_ix = sem("token_table_done")
        s_ixc = sem("token_table_copied")
        s_ovr = sem("overflow_table_ready")
        s_w1 = [sem(f"w1_loaded{s}") for s in range(RING)]
        s_w2 = [sem(f"w2_loaded{s}") for s in range(RING)]
        s_ixs = sem("result_rows_ready")
        s_idn = sem("index_copied")
        s_idm = sem("result_index_copied")
        s_xg = [sem(f"rows_gathered{s}") for s in range(XG)]
        s_xt = sem("rows_transposed")
        s_xtc = sem("rows_transpose_copied")
        s_gw = sem("gates_ready")
        s_gs = sem("gates_spread")
        s_gt = sem("gates_transposed")
        s_gtc = sem("gates_transpose_copied")
        s_gb = sem("gated_biases_done")
        s_g1 = sem("hidden_done")
        s_hnc = sem("hidden_copied")
        s_hT = sem("hidden_transposed")
        s_ha = sem("hidden_biased")
        s_hr = sem("hidden_ready")
        s_g2 = sem("result_done")
        s_yc = sem("result_copied")
        s_ys = [sem(f"result_stored{s}") for s in range(XG)]
        s_yo = sem("overflow_result_stored")
        s_all = sem("all_overflow_results_stored")
        s_yg = [sem(f"token_results_loaded{h}") for h in range(4)]
        s_o = sem("output_ready")
        s_out = sem("output_stored")

        block = ctx.enter_context(nc.Block())

        MAIN_X0, MAIN_W0 = -(-PAIRS // XG), -(-PAIRS // RING)
        over_slot = 0
        OVER_IDN = PAIRS % XG

        def xw_products(it):
            first = it - 2 + max(0, it - (HEAD - 2))
            count = 0 if it < 2 else 1 if it < HEAD - 2 else 2
            return [(u // 2, u % 2) for u in range(first, first + count)]

        def gated_bias(t):
            bank, at = ps[(3, 5, 7)[t // 2]], (t % 2) * D
            return bank[0:NP, at:at + D]

        def h_bank(layer, o, c):
            return ps[(4, 0)[layer] + 2 * o + c]

        def back_rows(t):
            return ps[(4 + t) % 8][0:NP, 0:D]

        def wait_for_results(eng):
            for slot in range(XG):
                eng.wait_ge(s_ys[slot], 16 * uses(0, PAIRS - 1, XG, (PAIRS - 1 - slot) % XG))

        PARTS_T = [(0, 3), (3, NT)]

        def load_results(eng, k, h, a, b):
            rows = y_dram[1 + k * NODES:1 + (k + 1) * NODES, :].rearrange("(p t) d -> p t d", t=NT)
            eng.dma_start(yg[:, k, a:b, :], rows[:, a:b, :]).then_inc(s_yg[2 * k + h], 16)

        @block.sync
        def _(sp):
            sp.dma_start(e_dst[:, :], dst.rearrange("(g e) -> g e", g=GROUPS)).then_inc(s_ed, 16)
            sp.dma_start(e_src[:, :], src.rearrange("(g e) -> g e", g=GROUPS)).then_inc(s_ed, 16)
            sp.dma_start(e_f[:, 2, :], ew.rearrange("(g e) -> g e", g=GROUPS)).then_inc(s_ed, 16)
            sp.dma_start(xs[:, :, :], x.rearrange("(p t) d -> p t d", t=NT)).then_inc(s_x, 16)
            sp.dma_start(epsb[:, :], eps.rearrange("(a b) -> a b", a=1).to_broadcast([128, 1])).then_inc(s_eps, 16)
            sp.dma_start(w1g[:, :, :], W1.rearrange("(k p) f -> p k f", k=2)).then_inc(s_par, 16)
            for n, v in enumerate((b1, g1, be1, b2, g2, be2)):
                sp.dma_start(vec[2 * n:2 * n + 2, :], v.rearrange("(o p) -> o p", o=2)).then_inc(s_vec, 16)
            sp.dma_start(w2g[:, :, :], W2.rearrange("(k p) f -> p k f", k=2)).then_inc(s_par, 16)
            sp.dma_start(wrs[:, :, :], Wr.rearrange("(k p) f -> p k f", k=2)).then_inc(s_rt, 16)
            for half in range(2):
                sp.dma_start(brT[half * EXPERTS:(half + 1) * EXPERTS, :], br.rearrange("(e a) -> e a", a=1)).then_inc(s_rt, 16)
            sp.dma_start(fb1s[:, :], fb1).then_inc(s_fb, 16)
            sp.dma_start(fb2s[:, :], fb2).then_inc(s_fb, 16)

            f1 = F1.rearrange("e (p k) f -> p e (k f)", k=2)
            f2 = F2.rearrange("e (p j) f -> p e (j f)", j=4)

            def load_w1(c, slot):
                sp.dma_start(w1r(slot), f1[:, bass.ds(c * 2, 2), :]).then_inc(s_w1[slot], 16)

            def load_w2(c, slot):
                sp.dma_start(w2r(slot), f2[:, bass.ds(c * 2, 2), :]).then_inc(s_w2[slot], 16)

            for c in range(OWN):
                load_w1(c, c)
                load_w2(c, c)
            sp.wait_ge(s_h, 4)
            for c in range(OWN, RING):
                load_w1(c, c)
            sp.wait_ge(s_xn, 2 * NT)
            for k in range(TOPK):
                sp.dma_start(xf_dram[1 + k * NODES:1 + (k + 1) * NODES, :].rearrange("(p t) d -> p (t d)", t=NT),
                             xn[:, :, :].rearrange("p t d -> p (t d)")).then_inc(s_xfd, 16)
            sp.dma_start(xf_dram[0:1, :], xn[0:1, 0, :]).then_inc(s_xfd, 16)
            sp.wait_ge(s_bi, 1)
            load_w2(OWN, OWN)
            sp.wait_ge(s_lh, 1)
            load_w2(OWN + 1, OWN + 1)

            def load_next(i, m):
                c = i * RING + m
                sp.wait_ge(s_g1, c - RING + 1)
                if m >= FIRST:
                    sp.wait_ge(s_w2[(m - AHEAD) % RING], uses(i, m, RING, AHEAD) * 16)
                load_w1(c, m % RING)
                if m > RING:
                    sp.wait_ge(s_g2, c - RING)
                    load_w2(c - 1, (m - 1) % RING)

            for m in range(RING, FIRST):
                load_next(0, m)
            with sp.Fori(0, (PAIRS - FIRST) // RING) as i:
                for m in range(FIRST, FIRST + RING):
                    load_next(i, m)
            sp.wait_ge(s_g2, PAIRS - RING)
            load_w2(PAIRS - 1, (PAIRS - 1) % RING)

            sp.wait_ge(s_ovr, 1)
            any_over = sp.value_load(oflag[0:1, 0:1], min_val=0, max_val=1)
            with sp.If(any_over):
                with sp.Fori(0, OVER_PAIRS) as j:
                    used = sp.value_load(oflag[0:1, bass.ds(j, 1)], min_val=0, max_val=1)
                    with sp.If(used):
                        sp.wait_ge(s_g1, j + PAIRS)
                        sp.wait_ge(s_g2, j + PAIRS)
                        for half in range(2):
                            e = sp.value_load(oexp[0:1, bass.ds(j * 2 + half, 1)], min_val=0, max_val=EXPERTS - 1)
                            sp.dma_start(w1r(over_slot)[:, half, :],
                                         f1[:, bass.ds(e, 1), :].rearrange("p a f -> p (a f)")).then_inc(s_w1[over_slot], 16)
                            sp.dma_start(w2r(over_slot)[:, half, :],
                                         f2[:, bass.ds(e, 1), :].rearrange("p a f -> p (a f)")).then_inc(s_w2[over_slot], 16)
                        sp.nop()
                sp.wait_ge(s_all, 1)
                sp.nop()

            wait_for_results(sp)
            for k in range(TOPK):
                load_results(sp, k, 0, *PARTS_T[0])
            sp.wait_ge(s_o, 1)
            sp.dma_start(out.rearrange("(p t) d -> p t d", t=NT)[:, 0:PARTS_T[0][1], :], os[:, 0:PARTS_T[0][1], :]).then_inc(s_out, 16)
            sp.wait_ge(s_out, 32)

        @block.gpsimd
        def _(pool):
            steps = [0]

            def link(ins):
                steps[0] += 1
                ins.then_inc(s_pool, 1)
                pool.wait_ge(s_pool, steps[0])

            pool.iota(iota_src[:, :, :], pattern=[[1, NT], [NT, 128]], base=0, channel_multiplier=0,
                      allow_small_or_imprecise_dtypes=True)
            pool.iota(iota_c[:, :], pattern=[[1, 128]], base=0, channel_multiplier=0,
                      allow_small_or_imprecise_dtypes=True).then_inc(s_cst, 1)
            pool.memset(bn_eps[:, :], EPS)
            link(pool.memset(ident[:, :], 0.0))
            pool.affine_select(out=ident[:, :], in_=ident[:, :], compare_op=ALU.not_equal, fill=1.0, base=0,
                               pattern=[[-1, 128]], channel_multiplier=1).then_inc(s_cst, 1)
            pool.iota(w64[:, :, :], pattern=[[WIN, ROUNDS], [0, GROUPS]], base=0, channel_multiplier=0,
                      allow_small_or_imprecise_dtypes=True).then_inc(s_cst, 1)
            link(pool.memset(AT[:, :, :], 0.0))
            pool.affine_select(out=AT[:, :, :], in_=AT[:, :, :], compare_op=ALU.not_equal, fill=1.0, base=0,
                                    pattern=[[1, NT], [-1, AT_W]], channel_multiplier=NT).then_inc(s_at0, 1)
            pool.wait_ge(s_eps, 16)
            pool.tensor_scalar(epsb[:, :], epsb[:, :], 1.0, None, ALU.add).then_inc(s_cst, 1)

            def more_constants():
                link(pool.memset(tri[:, :], 1.0))
                pool.affine_select(out=tri[:, :], in_=tri[:, :], compare_op=ALU.is_gt, fill=0.0, base=0,
                                   pattern=[[1, NP]], channel_multiplier=-1)
                pool.memset(ones_b[:, :], 1.0)
                pool.memset(n64[:, :], float(-CAP))
                pool.iota(e64b[:, :, :], pattern=[[0, NT], [CAP, EXPERTS]], base=0, channel_multiplier=0,
                          allow_small_or_imprecise_dtypes=True)
                pool.iota(e64s[:, :], pattern=[[CAP, EXPERTS]], base=-CAP * (EXPERTS - 1), channel_multiplier=0,
                          allow_small_or_imprecise_dtypes=True)
                pool.iota(tok[:, :], pattern=[[NODES, TOPK], [1, NT]], base=1, channel_multiplier=NT,
                          allow_small_or_imprecise_dtypes=True)
                pool.iota(spare[:, :], pattern=[[128, ALL_PAIRS]], base=ROWS, channel_multiplier=1,
                          allow_small_or_imprecise_dtypes=True)
                pool.iota(bi[:, :], pattern=[[CAP, 2 * OVER_PAIRS]], base=0, channel_multiplier=0,
                          allow_small_or_imprecise_dtypes=True)
                pool.iota(pi2[:, :], pattern=[[2 * CAP, OVER_PAIRS]], base=0, channel_multiplier=0,
                          allow_small_or_imprecise_dtypes=True).then_inc(s_cst, 1)

            more_constants()
            pool.wait_ge(s_ctl, 1)
            pool.wait_ge(s_at0, 2)

            def add_window(it, buf):
                if not isinstance(it, int) or it >= 1:
                    pool.wait_ge(s_at, it)
                base = pool.value_load(bases[0:1, bass.ds(it, 1)], min_val=0, max_val=NODES - 1)
                pool.wait_ge(s_awc, it + 1)
                win = AT[:, :, bass.ds(base, WIN)]
                pool.tensor_tensor(win, win, AWs[:, buf, :, :], ALU.add).then_inc(s_at, 1)

            for it in range(2):
                add_window(it, it)
            with pool.Fori(1, GROUPS // 2) as i:
                for buf in range(2):
                    add_window(i * 2 + buf, buf)
            any_more = pool.value_load(flags[0:1, 1:2], min_val=0, max_val=1)
            with pool.If(any_more):
                with pool.Fori(1, ROUNDS) as r:
                    more = pool.value_load(flags[0:1, bass.ds(r, 1)], min_val=0, max_val=1)
                    with pool.If(more):
                        with pool.Fori(0, GROUPS // 2) as i:
                            for buf in range(2):
                                add_window(r * GROUPS + i * 2 + buf, buf)
                        pool.nop()
                pool.nop()

            pool.wait_ge(s_gw, 1)
            for k, g in enumerate((lg, G1)):
                ins = pool.tensor_tensor(g[:, :, :], Sel[:, k, :, :], gt[:, 3 + k, :].unsqueeze(2).to_broadcast([NP, NT, EXPERTS]), ALU.mult)
            link(ins)
            pool.tensor_tensor(lg[:, :, :], lg[:, :, :], G1[:, :, :], ALU.add).then_inc(s_gs, 1)

            def copy_index(c, s):
                pool.tensor_copy(idn[:, s:s + 1], idx[:, bass.ds(c, 1)]).then_inc(s_idn, 1)

            def copy_result_index(c, s):
                pool.tensor_copy(idm[:, s:s + 1], ids[:, bass.ds(c, 1)]).then_inc(s_idm, 1)

            def gather(s, column=None):
                at = s if column is None else column
                pool.indirect_dma_start(out=xg[:, s, :], out_offset=None, in_=xf_dram,
                                        in_offset=bass.IndirectOffsetOnAxis(ap=idn[:, at:at + 1], axis=0),
                                        bounds_check=ROWS - 1).then_inc(s_xg[s], 16)

            def scatter(s, stored):
                pool.indirect_dma_start(out=y_dram, out_offset=bass.IndirectOffsetOnAxis(ap=idm[:, s:s + 1], axis=0),
                                        in_=ys[:, s, :], in_offset=None,
                                        bounds_check=ROWS + ALL_PAIRS * 128 - 1).then_inc(stored, 16)

            def step(i, m):
                c = i * RING + m
                if m >= XG:
                    pool.wait_ge(s_xt, c - XG + 1)
                if m >= XG - 1:
                    pool.wait_ge(s_xg[(m + 1) % XG], uses(i, m, XG, XG - 1) * 16)
                pool.wait_ge(s_idn, c + 1)
                if m >= LAG:
                    pool.wait_ge(s_yc, c - LAG + 1)
                    pool.wait_ge(s_idm, c - LAG + 1)
                if m >= LAG - 1 + XG:
                    pool.wait_ge(s_ys[(m - LAG + 1) % XG], uses(i, m, XG, LAG - 1 + XG) * 16)
                copy_index(c + 1, (m + 1) % XG)
                if m >= LAG - 1:
                    copy_result_index(c - LAG + 1, (m - LAG + 1) % XG)
                gather(m % XG)
                if m >= LAG:
                    scatter((m - LAG) % XG, s_ys[(m - LAG) % XG])

            pool.wait_ge(s_ixc, 1)
            copy_index(0, 0)
            pool.wait_ge(s_xfd, 48)
            for m in range(FIRST):
                if m == LAG - 1:
                    pool.wait_ge(s_ixs, 1)
                step(0, m)
            with pool.Fori(0, (PAIRS - FIRST) // RING) as i:
                for m in range(FIRST, FIRST + RING):
                    step(i, m)
            for c in range(PAIRS - LAG, PAIRS):
                if c + 1 < PAIRS:
                    pool.wait_ge(s_ys[(c + 1) % XG], (c + 1) // XG * 16)
                    copy_result_index(c + 1, (c + 1) % XG)
                pool.wait_ge(s_yc, c + 1)
                pool.wait_ge(s_idm, c + 1)
                scatter(c % XG, s_ys[c % XG])
            pool.wait_ge(s_ovr, 1)
            any_over = pool.value_load(oflag[0:1, 0:1], min_val=0, max_val=1)
            with pool.If(any_over):
                pool.wait_ge(s_ys[over_slot], 16 * MAIN_X0)
                pool.wait_ge(s_idn, PAIRS + 1)
                with pool.Fori(0, OVER_PAIRS) as j:
                    used = pool.value_load(oflag[0:1, bass.ds(j, 1)], min_val=0, max_val=1)
                    with pool.If(used):
                        pool.wait_ge(s_xt, j + PAIRS)
                        copy_index(j + PAIRS, OVER_IDN)
                        copy_result_index(j + PAIRS, over_slot)
                        pool.wait_ge(s_idn, j + PAIRS + 2)
                        pool.wait_ge(s_idm, j + PAIRS + 1)
                    with pool.If(used):
                        gather(over_slot, OVER_IDN)
                        pool.wait_ge(s_yc, j + PAIRS + 1)
                    with pool.If(used):
                        scatter(over_slot, s_yo)
                        pool.wait_ge(s_yo, (j + 1) * 16)
                        pool.nop()
                pool.memset(done[:, :], 0.0).then_inc(s_all, 1)
                pool.nop()

        @block.scalar
        def _(act):
            act.wait_ge(s_cst, 2)
            act.wait_ge(s_var, 1)
            act.activation(nrm[0:NP, 4, :], mv[0:NP, :, 1], ACT.Sqrt, bias=bn_eps[0:NP, :]).then_inc(s_std, 1)
            act.wait_ge(s_cst, 4)
            act.wait_ge(s_at0, 1)
            act.activation(AT[:, :, :], AT[:, :, :], ACT.Copy, scale=epsb[:, 0:1]).then_inc(s_at0, 1)
            act.wait_ge(s_vt, 1)
            act.activation(vecT[:, :], ps[7][:, 0:NVEC], ACT.Copy).then_inc(s_vc, 1)
            act.wait_ge(s_ctl, 1)

            def last_quad(it, buf):
                f = EFs[:, (buf * 5 + 1) * QUADS - 1:(buf * 5 + 1) * QUADS]
                if not isinstance(it, int) or it >= 1:
                    act.wait_ge(s_oha, it)
                if not isinstance(it, int) or it >= 2:
                    act.wait_ge(s_aw, it - 1)
                act.wait_ge(s_efs, it + 1)
                act.activation(sabs[:, :], iota_src[0:EP, :, :].rearrange("p t n -> p (t n)"), ACT.Abs, bias=f,
                               scale=-1.0).then_inc(s_sa, 1)
                act.wait_ge(s_sa, it + 1)
                act.activation(S[:, buf, QUADS - 1, :], sabs[:, :], ACT.Relu, bias=1.0, scale=-1.0).then_inc(s_oha, 1)

            def copy_window(it, buf):
                if not isinstance(it, int) or it >= 2:
                    act.wait_ge(s_at, it - 1)
                act.wait_ge(s_aw, it + 1)
                act.activation(AWs[:, buf, :, :], ps[buf][:, 0:NT * WIN].rearrange("p (s w) -> p s w", s=NT),
                               ACT.Copy).then_inc(s_awc, 1)

            for it in range(2):
                last_quad(it, it)
            for it in range(HEAD):
                copy_window(it, it % 2)
                for t, k in xw_products(it):
                    if k == 1:
                        act.wait_ge(s_xw, t + 1)
                        act.activation(xw[:, t, :], ps[4 + t % 2][0:NP, 0:D], ACT.Copy).then_inc(s_xwc, 1)
                if it == 1:
                    for t in range(NT):
                        act.wait_ge(s_nt, t + 1)
                        act.activation(nT[:, :, t * NP:(t + 1) * NP],
                                       ps[2 + t % 2][:, 0:2 * NP].rearrange("p (k n) -> p k n", k=2), ACT.Copy).then_inc(s_ntc, 1)
                last_quad(it + 2, it % 2)
            with act.Fori(HEAD // 2, GROUPS // 2 - 1) as i:
                for buf in range(2):
                    copy_window(i * 2 + buf, buf)
                    last_quad(i * 2 + buf + 2, buf)
            for it in range(GROUPS - 2, GROUPS):
                copy_window(it, it % 2)
            any_more = act.value_load(flags[0:1, 1:2], min_val=0, max_val=1)
            with act.If(any_more):
                with act.Fori(1, ROUNDS) as r:
                    more = act.value_load(flags[0:1, bass.ds(r, 1)], min_val=0, max_val=1)
                    with act.If(more):
                        with act.Fori(0, GROUPS // 2) as i:
                            for buf in range(2):
                                it = r * GROUPS + i * 2 + buf
                                last_quad(it, buf)
                                copy_window(it, buf)
                        act.nop()
                act.nop()

            for layer in range(2):
                for m, (o, c) in enumerate(((0, 0), (0, 1), (1, 0))):
                    a, b = CHUNKS[c]
                    if c == 0:
                        act.wait_ge(s_var, 2 + 2 * layer + o)
                        act.activation(nrm[:, 4, o:o + 1], mv[:, o, 1:2], ACT.Sqrt, bias=bn_eps[:, :]).then_inc(s_std, 1)
                        act.wait_ge(s_bn, 2 * layer + o + 1)
                    act.activation((nT, hT)[layer][:, o, a:b], h_bank(layer, o, c)[:, 0:b - a], ACT.Identity,
                                   bias=nrm[:, 3, o:o + 1], scale=nrm[:, 1, o:o + 1]).then_inc(s_hn, 1)
            act.wait_ge(s_var, 6)
            act.activation(nrm[0:NP, 4, :], mv[0:NP, :, 1], ACT.Sqrt, bias=bn_eps[0:NP, :]).then_inc(s_std, 1)
            for t in range(NT):
                act.wait_ge(s_nt, NT + t + 1)
                act.activation(nT[:, :, t * NP:(t + 1) * NP],
                               ps[t % 2][:, 0:2 * NP].rearrange("p (k n) -> p k n", k=2), ACT.Copy).then_inc(s_ntc, 1)
            act.wait_ge(s_rt, 48)
            for half in range(2):
                rows, width = slice(half * EXPERTS, (half + 1) * EXPERTS), (3 - half) * NP
                act.wait_ge(s_lg, 1)
                act.activation(lgT[rows, 0:width], ps[3][rows, 0:width], ACT.Identity, bias=brT[rows, :]).then_inc(s_lgc, 1)
            act.wait_ge(s_ld, 1)
            act.activation(gt[:, 1, :], gt[:, 0, :], ACT.Exp).then_inc(s_le, 1)

            act.wait_ge(s_bi, 1)
            act.activation(b1T[:, :, :], ps[6][:, 0:4 * EXPERTS].rearrange("p (j e) -> p j e", j=4), ACT.Copy).then_inc(s_bic, 1)
            act.wait_ge(s_gt, 1)
            act.activation(GT[:, 0:4 * NP], ps[0][0:EXPERTS, 0:4 * NP], ACT.Copy)
            act.activation(GT[:, 4 * NP:NODES], ps[1][0:EXPERTS, 0:NP], ACT.Copy).then_inc(s_gtc, 1)

            def copy_rows(c, par):
                act.wait_ge(s_xt, c + 1)
                act.activation(xgT[:, par, :, :], ps[par][:, 0:256].rearrange("p (k n) -> p k n", k=2),
                               ACT.Copy).then_inc(s_xtc, 1)

            def relu(c, par):
                act.wait_ge(s_ha, c + 1)
                act.activation(hr[:, par, :, :], hb[:, :, :], ACT.Relu).then_inc(s_hr, 1)

            def step(i, m):
                c = i * RING + m
                if m >= 2:
                    act.wait_ge(s_g1, c - 1)
                copy_rows(c, m % 2)
                if m >= 1:
                    if m >= 3:
                        act.wait_ge(s_g2, c - 2)
                    relu(c - 1, (m - 1) % 2)

            for m in range(FIRST):
                step(0, m)
            with act.Fori(0, (PAIRS - FIRST) // RING) as i:
                for m in range(FIRST, FIRST + RING):
                    step(i, m)
            act.wait_ge(s_g2, PAIRS - 2)
            relu(PAIRS - 1, (PAIRS - 1) % 2)

            act.wait_ge(s_ovr, 1)
            any_over = act.value_load(oflag[0:1, 0:1], min_val=0, max_val=1)
            with act.If(any_over):
                with act.Fori(0, OVER_PAIRS) as j:
                    used = act.value_load(oflag[0:1, bass.ds(j, 1)], min_val=0, max_val=1)
                    with act.If(used):
                        c = j + PAIRS
                        act.wait_ge(s_yc, c)
                        copy_rows(c, 0)
                        relu(c, 0)
                        act.nop()
                act.wait_ge(s_all, 1)
                act.nop()
            wait_for_results(act)
            for k in range(TOPK):
                load_results(act, k, 1, *PARTS_T[1])
            act.wait_ge(s_o, 2)
            act.dma_start(out.rearrange("(p t) d -> p t d", t=NT)[:, PARTS_T[1][0]:NT, :], os[:, PARTS_T[1][0]:NT, :]).then_inc(s_out, 16)

        @block.vector
        def _(dve):
            steps = [0]

            def link(ins):
                steps[0] += 1
                ins.then_inc(s_dve, 1)
                dve.wait_ge(s_dve, steps[0])

            def layer_norm_factors(count):
                var, sd, r, t = mv[0:NP, :, 1], nrm[0:NP, 4, :], nrm[0:NP, 0, :], nrm[0:NP, 5, :]
                v = nrm[0:NP, 1, :]
                dve.tensor_scalar(v, var, EPS, None, ALU.add)
                dve.wait_ge(s_std, count)
                link(dve.reciprocal(r, sd))
                link(dve.tensor_tensor(t, r, r, ALU.mult))
                link(dve.scalar_tensor_tensor(out=t, in0=t, scalar=-0.5, in1=v, op0=ALU.mult, op1=ALU.mult))
                dve.scalar_tensor_tensor(out=r, in0=t, scalar=1.5, in1=r, op0=ALU.add, op1=ALU.mult).then_inc(s_lnf, 1)

            def batch_norm_factors(o, layer, count):
                r, gain, diff, shift, sd, t = (nrm[:, k, o:o + 1] for k in range(6))
                bias, gamma, beta = (vecT[:, 6 * layer + 2 * k + o:6 * layer + 2 * k + o + 1] for k in range(3))
                v = mv[:, 2 + o, 0:1]
                dve.tensor_scalar(v, mv[:, o, 1:2], EPS, None, ALU.add)
                link(dve.tensor_tensor(diff, mv[:, o, 0:1], bias, ALU.add))
                dve.tensor_tensor(diff, bias, diff, ALU.subtract)
                dve.wait_ge(s_std, count)
                link(dve.reciprocal(r, sd))
                link(dve.scalar_tensor_tensor(out=t, in0=r, scalar=v, in1=r, op0=ALU.mult, op1=ALU.mult))
                link(dve.tensor_scalar(t, t, -0.5, 1.5, ALU.mult, ALU.add))
                link(dve.scalar_tensor_tensor(out=gain, in0=r, scalar=t, in1=gamma, op0=ALU.mult, op1=ALU.mult))
                dve.scalar_tensor_tensor(out=shift, in0=diff, scalar=gain, in1=beta, op0=ALU.mult, op1=ALU.add).then_inc(s_bn, 1)

            dve.wait_ge(s_ed, 48)
            dve.tensor_copy(e_f[:, 0, :], e_src[:, :])
            link(dve.tensor_copy(e_f[:, 1, :], e_dst[:, :]))
            dve.tensor_reduce(dlo[:, 1:2], e_f[:, 1, :], AX.X, ALU.max)
            link(dve.tensor_reduce(dlo[:, 0:1], e_f[:, 1, :], AX.X, ALU.min))
            dve.tensor_tensor(dlo[:, 2:3], dlo[:, 1:2], dlo[:, 0:1], ALU.subtract)
            dve.tensor_scalar(e_f[:, 1, :], e_f[:, 1, :], dlo[:, 0:1], None, ALU.subtract).then_inc(s_ef, 1)
            dve.wait_ge(s_x, 16)
            for t in range(NT):
                ins = dve.bn_stats(st[0:NP, t, :], xs[:, t, :])
            link(ins)
            for t in range(NT):
                ins = dve.bn_aggr(mv[0:NP, t, :], st[0:NP, t, :])
            ins.then_inc(s_var, 1)
            dve.wait_ge(s_et, 1)
            et = ps[6][0:EP, 0:3 * QUADS * GROUPS].rearrange("p (c g) -> p g c", g=GROUPS)
            link(dve.tensor_copy(EF[:, :, 0:3 * QUADS], et))
            w = [EF[:, :, (2 + k) * QUADS:(3 + k) * QUADS] for k in range(PARTS)]
            wbv = wb[:, :].rearrange("p (g q) -> p g q", g=GROUPS)
            for k in range(1, PARTS):
                link(dve.tensor_copy(wbv, w[k - 1]))
                link(dve.tensor_tensor(w[k], w[k - 1], wbv, ALU.subtract))
            link(dve.tensor_copy(drow[:, :], ps[7][0:1, 64:64 + 2 * GROUPS]))
            link(dve.tensor_reduce(span[:, :], drow[0:1, GROUPS:2 * GROUPS], AX.X, ALU.max))
            dve.wait_ge(s_cst, 3)
            link(dve.tensor_scalar(flags[:, :], w64[:, :, 0], span[0:1, 0:1], None, ALU.is_le))
            link(dve.tensor_tensor(w64[:, :, :], w64[:, :, :],
                                   drow[0:1, 0:GROUPS].unsqueeze(1).to_broadcast([1, ROUNDS, GROUPS]), ALU.add))
            dve.tensor_scalar(bases[:, :], w64[:, :, :].rearrange("p r g -> p (r g)"), float(NODES - 1), None,
                              ALU.min).then_inc(s_ctl, 1)
            dve.wait_ge(s_ctl, 1)

            def onehots(it, buf, meanwhile=None):
                sources, destinations, weights = (EFs[:, (buf * 5 + k) * QUADS:(buf * 5 + n) * QUADS]
                                                  for k, n in ((0, 1), (1, 2), (2, 2 + PARTS)))
                shape = [EP, QUADS, WIN]
                dve.tensor_tensor(dhot[:, buf, :, :], iota_c[0:EP, 0:WIN].unsqueeze(1).to_broadcast(shape),
                                  destinations.unsqueeze(2).to_broadcast(shape), ALU.is_equal).then_inc(s_dh, 1)
                for q in range(QUADS - 1):
                    dve.tensor_scalar(S[:, buf, q, :], iota_src[0:EP, :, :].rearrange("p t n -> p (t n)"),
                                      sources[:, q:q + 1], None, ALU.is_equal)
                    if q == 0 and meanwhile:
                        meanwhile()
                dve.wait_ge(s_dh, it + 1)
                shape = [EP, QUADS, PARTS, WIN]
                dve.tensor_tensor(Dw[:, buf, :, :, :], dhot[:, buf, :, :].unsqueeze(2).to_broadcast(shape),
                                  weights.rearrange("p (k q) -> p q k", k=PARTS).unsqueeze(3).to_broadcast(shape),
                                  ALU.mult).then_inc(s_oh, 1)

            def copy_fields(g, it, buf):
                if not isinstance(it, int) or it >= 2:
                    dve.wait_ge(s_oh, it - 1)
                    dve.wait_ge(s_oha, it - 1)
                dve.tensor_copy(EFs[:, buf * 5 * QUADS:(buf + 1) * 5 * QUADS],
                                EF[:, bass.ds(g, 1), :].rearrange("p g c -> p (g c)")).then_inc(s_efs, 1)

            def one_group(it, buf, more=True):
                if not isinstance(it, int) or it >= 2:
                    dve.wait_ge(s_aw, it - 1)
                dve.wait_ge(s_efs, it + 1)
                onehots(it, buf, (lambda: copy_fields(it + 1, it + 1, 1 - buf)) if more else None)

            dve.wait_ge(s_ef, 1)
            copy_fields(0, 0, 0)
            for it in range(2):
                one_group(it, it)
            layer_norm_factors(1)
            dve.wait_ge(s_lnf, 1)
            for t in range(NT):
                dve.tensor_scalar(xn[:, t, :], xs[:, t, :], mv[0:NP, t, 0:1], nrm[0:NP, 0, t:t + 1],
                                  ALU.subtract, ALU.mult).then_inc(s_xn, 1)
            with dve.Fori(1, GROUPS // 2 - 1) as i:
                for buf in range(2):
                    one_group(i * 2 + buf, buf)
            for it in range(GROUPS - 2, GROUPS):
                one_group(it, it % 2, it + 1 < GROUPS)
            any_more = dve.value_load(flags[0:1, 1:2], min_val=0, max_val=1)
            with dve.If(any_more):
                with dve.Fori(1, ROUNDS) as r:
                    more = dve.value_load(flags[0:1, bass.ds(r, 1)], min_val=0, max_val=1)
                    with dve.If(more):
                        dve.tensor_scalar(EF[:, :, QUADS:2 * QUADS], EF[:, :, QUADS:2 * QUADS], float(WIN), None,
                                          ALU.subtract).then_inc(s_ef, 1)
                        with dve.Fori(0, GROUPS // 2) as i:
                            for buf in range(2):
                                it = r * GROUPS + i * 2 + buf
                                dve.wait_ge(s_ef, r + 1)
                                copy_fields(i * 2 + buf, it, buf)
                                one_group(it, buf, False)
                        dve.nop()
                dve.nop()

            for layer in range(2):
                for o in range(2):
                    for c, (a, b) in enumerate(CHUNKS):
                        dve.wait_ge(s_h, 4 * layer + 2 * o + c + 1)
                        ins = dve.bn_stats(st[:, 2 * o + c, :], h_bank(layer, o, c)[:, 0:b - a])
                    link(ins)
                    dve.bn_aggr(mv[:, o, :], st[:, 2 * o:2 * o + 2, :]).then_inc(s_var, 1)
                    if layer == 0 and o == 0:
                        dve.wait_ge(s_vc, 1)
                    dve.wait_ge(s_var, 2 + 2 * layer + o)
                    batch_norm_factors(o, layer, 2 + 2 * layer + o)
                a, b = CHUNKS[1]
                dve.wait_ge(s_bn, 2 * layer + 2)
                dve.tensor_scalar((nT, hT)[layer][:, 1, a:b], h_bank(layer, 1, 1)[:, 0:b - a], nrm[:, 1, 1:2],
                                  nrm[:, 3, 1:2], ALU.mult, ALU.add).then_inc(s_hd, 1)
            for t in range(NT + 1):
                if t < NT:
                    dve.wait_ge(s_bt, t + 1)
                    dve.tensor_tensor(x1[:, t, :], back_rows(t), xs[:, t, :], ALU.add).then_inc(s_x1, 1)
                if t >= 1:
                    dve.wait_ge(s_x1, t)
                    ins = dve.bn_stats(st[0:NP, t - 1, :], x1[:, t - 1, :])
            link(ins)
            for t in range(NT):
                ins = dve.bn_aggr(mv[0:NP, t, :], st[0:NP, t, :])
            ins.then_inc(s_var, 1)
            dve.wait_ge(s_var, 6)
            layer_norm_factors(6)
            dve.wait_ge(s_lnf, 2)
            for t in range(NT):
                dve.tensor_scalar(xn[:, t, :], x1[:, t, :], mv[0:NP, t, 0:1], nrm[0:NP, 0, t:t + 1],
                                  ALU.subtract, ALU.mult).then_inc(s_xn, 1)

            dve.wait_ge(s_lt, 1)
            logits = [ps[2][0:NP, 2 * (t % 3) * EXPERTS + t // 3 * EXPERTS:][:, 0:EXPERTS] for t in range(NT)]
            for t in range(NT):
                ins = dve.max(m8[:, t, :], logits[t])
            link(ins)
            for t in range(NT):
                ins = dve.max_index(i8[:, t, :], m8[:, t, :], logits[t])
            dve.tensor_tensor(gt[:, 0, :], m8[:, :, 1], m8[:, :, 0], ALU.subtract).then_inc(s_ld, 1)
            dve.wait_ge(s_ld, 1)
            link(dve.tensor_copy(ixf[:, :, :], i8[:, :, 0:TOPK].rearrange("p t k -> p k t")))
            dve.wait_ge(s_cst, 5)
            experts = iota_c[0:NP, 0:EXPERTS].unsqueeze(1).to_broadcast([NP, TOPK * NT, EXPERTS])
            link(dve.tensor_tensor(Sel[:, :, :, :].rearrange("p k t e -> p (k t) e"), experts,
                                   ixf[:, :, :].rearrange("p k t -> p (k t)").unsqueeze(2).to_broadcast([NP, TOPK * NT, EXPERTS]),
                                   ALU.is_equal))
            dve.tensor_tensor(Mb[:, :, :], Sel[:, 0, :, :], Sel[:, 1, :, :], ALU.add).then_inc(s_m, 1)
            dve.wait_ge(s_le, 1)
            link(dve.tensor_scalar(gt[:, 2, :], gt[:, 1, :], 1.0, None, ALU.add))
            link(dve.reciprocal(gt[:, 3, :], gt[:, 2, :]))
            dve.tensor_tensor(gt[:, 4, :], gt[:, 1, :], gt[:, 3, :], ALU.mult).then_inc(s_gw, 1)
            dve.wait_ge(s_rk, 1)
            link(dve.tensor_scalar(cnt_i[:, :], ps[7][0:NP, NT * EXPERTS:(NT + 1) * EXPERTS], float(CAP - 1), None, ALU.add))
            link(dve.tensor_scalar(blk_i[:, :], cnt_i[:, :], 6, 6, ALU.arith_shift_right, ALU.arith_shift_left))
            link(dve.tensor_scalar(ov[:, :], blk_i[:, :], float(CAP), 0.0, ALU.subtract, ALU.max))
            link(dve.tensor_tensor_scan(cum[:, :], ov[:, :], n64[:, :], float(CAP * EXPERTS), ALU.add, ALU.add))
            link(dve.tensor_tensor(dlt[:, :], cum[:, :], ov[:, :], ALU.subtract))

            def tiles(bank):
                return ps[bank][0:NP, 0:NT * EXPERTS].rearrange("p (t e) -> p t e", t=NT)

            link(dve.scalar_tensor_tensor(out=slm[:, :, :], in0=tiles(7), scalar=float(CAP),
                                          in1=dlt[:, :].unsqueeze(1).to_broadcast([NP, NT, EXPERTS]),
                                          op0=ALU.is_ge, op1=ALU.mult))
            dve.wait_ge(s_rk, 2)
            link(dve.tensor_tensor(slm[:, :, :], slm[:, :, :], tiles(4), ALU.add))
            link(dve.tensor_tensor(sly[:, :, :, :], slm[:, :, :].unsqueeze(1).to_broadcast([NP, TOPK, NT, EXPERTS]),
                                   Sel[:, :, :, :], ALU.mult))
            link(dve.tensor_reduce(slf[:, :], sly[:, :, :, :].rearrange("p k t e -> p (k t) e"), AX.X, ALU.add))
            link(dve.tensor_copy(sli[:, :], slf[:, :]))
            dve.tensor_scalar(lohi[:, 0, :], sli[:, :], 127, None, ALU.bitwise_and)
            link(dve.tensor_scalar(lohi[:, 1, :], sli[:, :], 7, None, ALU.logical_shift_right))
            link(dve.tensor_copy(lhf[:, :, :], lohi[:, :, :]))
            choices_pairs = [NP, TOPK * NT, ALL_PAIRS]
            link(dve.tensor_tensor(HI[:, :, :], iota_c[0:NP, 0:ALL_PAIRS].unsqueeze(1).to_broadcast(choices_pairs),
                                   lhf[:, 1, :].unsqueeze(2).to_broadcast(choices_pairs), ALU.is_equal))
            dve.tensor_tensor(HI[:, :, :], HI[:, :, :], tok[:, :].unsqueeze(2).to_broadcast(choices_pairs), ALU.mult)
            for m in range(TOPK * NT):
                dve.tensor_scalar(LO[:, m, :], iota_c[0:NP, :], lhf[:, 0, m:m + 1], None, ALU.is_equal).then_inc(s_lh, 1)
            dve.wait_ge(s_ix, 1)
            rows = ps[5][:, 0:ALL_PAIRS]
            dve.tensor_copy(idx[:, :], rows).then_inc(s_ixc, 1)
            link(dve.scalar_tensor_tensor(out=dsf[:, :], in0=rows, scalar=0.0, in1=spare[:, :],
                                          op0=ALU.is_equal, op1=ALU.mult))
            dve.tensor_tensor(ids[:, :], dsf[:, :], rows, ALU.add).then_inc(s_ixs, 1)
            dve.wait_ge(s_bic, 1)

            def bias_hidden(c, par, bias):
                dve.wait_ge(s_hT, c + 1)
                dve.tensor_tensor(hb[:, :, :].rearrange("p j (h n) -> p j h n", h=2),
                                  ps[4 + par][:, 0:512].rearrange("p (j h n) -> p j h n", j=4, h=2),
                                  bias.unsqueeze(3).to_broadcast([128, 4, 2, CAP]), ALU.add).then_inc(s_ha, 1)

            def copy_hidden(c, par):
                dve.wait_ge(s_g1, c + 1)
                dve.tensor_copy(hn[:, par, :], ps[2 + par][:, 0:HID]).then_inc(s_hnc, 1)

            def copy_result(c, par, slot):
                dve.wait_ge(s_g2, c + 1)
                dve.tensor_copy(ys[:, slot, :], ps[6 + par][:, 0:D]).then_inc(s_yc, 1)

            def step(i, m):
                c = i * RING + m
                if m >= 1:
                    if m >= 2:
                        dve.wait_ge(s_hr, c - 1)
                    bias_hidden(c - 1, (m - 1) % 2, b1T[:, :, bass.ds(c * 2 - 2, 2)])
                copy_hidden(c, m % 2)
                if m >= 1:
                    if m > XG:
                        dve.wait_ge(s_ys[(m - 1) % XG], uses(i, m, XG, XG + 1) * 16)
                    copy_result(c - 1, (m - 1) % 2, (m - 1) % XG)

            def overflow_table(part):
                half = slice(part % 2 * OVER_PAIRS, (part % 2 + 1) * OVER_PAIRS)
                shape = [1, OVER_PAIRS, EXPERTS]
                if part == 0:
                    link(dve.tensor_scalar(oflag[:, :], pi2[:, :], cum[0:1, EXPERTS - 1:EXPERTS], None, ALU.is_lt))
                    link(dve.tensor_tensor(cum[0:1, :], cum[0:1, :], e64s[:, :], ALU.add))
                if part < 2:
                    link(dve.tensor_tensor(ocmp[:, half, :], bi[0:1, half].unsqueeze(2).to_broadcast(shape),
                                           cum[0:1, :].unsqueeze(1).to_broadcast(shape), ALU.is_ge))
                elif part < 4:
                    link(dve.tensor_reduce(oexp_f[:, half], ocmp[:, half, :], AX.X, ALU.add))
                else:
                    dve.tensor_scalar(oexp[:, :], oexp_f[:, :], float(EXPERTS - 1), None, ALU.min).then_inc(s_ovr, 1)

            for m in range(FIRST):
                step(0, m)
                if 3 <= m < 8:
                    overflow_table(m - 3)
            with dve.Fori(0, (PAIRS - FIRST) // RING) as i:
                for m in range(FIRST, FIRST + RING):
                    step(i, m)
            last = PAIRS - 1
            dve.wait_ge(s_hr, last)
            bias_hidden(last, last % 2, b1T[:, :, 2 * last:2 * last + 2])
            dve.wait_ge(s_ys[last % XG], uses(0, last, XG, XG) * 16)
            copy_result(last, last % 2, last % XG)
            any_over = dve.value_load(oflag[0:1, 0:1], min_val=0, max_val=1)
            with dve.If(any_over):
                dve.wait_ge(s_ys[over_slot], MAIN_X0 * 16)
                with dve.Fori(0, OVER_PAIRS) as j:
                    used = dve.value_load(oflag[0:1, bass.ds(j, 1)], min_val=0, max_val=1)
                    with dve.If(used):
                        c = j + PAIRS
                        dve.wait_ge(s_ha, c)
                        for half in range(2):
                            e = dve.value_load(oexp[0:1, bass.ds(j * 2 + half, 1)], min_val=0, max_val=EXPERTS - 1)
                            ins = dve.tensor_copy(b1o[:, :, half:half + 1], b1T[:, :, bass.ds(e, 1)])
                        ins.then_inc(s_vc, 1)
                        copy_hidden(c, 0)
                        dve.wait_ge(s_vc, j + 2)
                        bias_hidden(c, 0, b1o[:, :, :])
                        copy_result(c, 0, over_slot)
                        dve.nop()
                dve.nop()
            dve.wait_ge(s_gb, 1)
            for t in range(NT):
                dve.tensor_tensor(x1[:, t, :], x1[:, t, :], gated_bias(t), ALU.add).then_inc(s_x1, 1)
            dve.wait_ge(s_x1, 2 * NT)
            for h, (a, b) in enumerate(PARTS_T):
                dve.wait_ge(s_yg[h], 16)
                for t in range(a, b):
                    ins = dve.scalar_tensor_tensor(out=acc[:, t, :], in0=yg[:, 0, t, :], scalar=gt[:, 3, t:t + 1],
                                                   in1=x1[:, t, :], op0=ALU.mult, op1=ALU.add)
            link(ins)
            for h, (a, b) in enumerate(PARTS_T):
                dve.wait_ge(s_yg[2 + h], 16)
                for t in range(a, b):
                    ins = dve.scalar_tensor_tensor(out=os[:, t, :], in0=yg[:, 1, t, :], scalar=gt[:, 4, t:t + 1],
                                                   in1=acc[:, t, :], op0=ALU.mult, op1=ALU.add)
                ins.then_inc(s_o, 1)

        @block.tensor
        def _(pe):
            mm, idt = pe.matmul, ident

            def keep_warm(bank, count):
                for _ in range(count):
                    mm(ps[bank][:, 384:512], idt[:, :], idt[:, :], start=True, stop=True)

            pe.wait_ge(s_cst, 2)
            pe.wait_ge(s_ef, 1)
            for k, col in enumerate((0, 2)):
                pe.transpose(ps[7][0:1, 64 + k * GROUPS:64 + (k + 1) * GROUPS], dlo[:, col:col + 1], idt[0:GROUPS, 0:GROUPS])
            for f in range(3):
                for q in range(QUADS):
                    m = f * QUADS + q
                    ins = pe.transpose(ps[6][0:EP, m * GROUPS:(m + 1) * GROUPS], e_f[:, f, q * EP:(q + 1) * EP],
                                       idt[0:GROUPS, 0:GROUPS])
            ins.then_inc(s_et, 1)
            pe.wait_ge(s_ctl, 1)
            pe.wait_ge(s_vec, 96)
            pe.transpose(ps[7][:, 0:NVEC], vec[:, :], idt[0:NVEC, 0:NVEC]).then_inc(s_vt, 1)
            def group(it, buf):
                pe.wait_ge(s_oh, it + 1)
                pe.wait_ge(s_oha, it + 1)
                for s in range(NT):
                    for q in range(QUADS):
                        for k in range(PARTS):
                            ins = mm(ps[buf][:, s * WIN:(s + 1) * WIN], S[:, buf, q, s * 128:(s + 1) * 128],
                                     Dw[:, buf, q, k, :], start=(q == 0 and k == 0),
                                     stop=(q == QUADS - 1 and k == PARTS - 1))
                ins.then_inc(s_aw, 1)

            keep_warm(4, WARM[0])
            for it in range(HEAD):
                if it >= 2:
                    pe.wait_ge(s_awc, it - 1)
                group(it, it % 2)
                if it == 1:
                    for t in range(NT):
                        pe.wait_ge(s_xn, t + 1)
                        if t >= 2:
                            pe.wait_ge(s_ntc, t - 1)
                        for k in range(2):
                            ins = pe.transpose(ps[2 + t % 2][:, k * NP:(k + 1) * NP], xn[:, t, k * 128:(k + 1) * 128],
                                               idt[0:NP, 0:NP])
                        ins.then_inc(s_nt, 1)
                    pe.wait_ge(s_par, 32)
                for t, k in xw_products(it):
                    if k == 0:
                        pe.wait_ge(s_ntc, t + 1)
                        if t >= 2:
                            pe.wait_ge(s_xwc, t - 1)
                    ins = mm(ps[4 + t % 2][0:NP, 0:D], nT[:, k, t * NP:(t + 1) * NP], w1g[:, k, :],
                             start=(k == 0), stop=(k == 1))
                    if k == 1:
                        ins.then_inc(s_xw, 1)
            with pe.Fori(HEAD // 2, GROUPS // 2) as i:
                for buf in range(2):
                    pe.wait_ge(s_awc, i * 2 + buf - 1)
                    group(i * 2 + buf, buf)
            any_more = pe.value_load(flags[0:1, 1:2], min_val=0, max_val=1)
            with pe.If(any_more):
                with pe.Fori(1, ROUNDS) as r:
                    more = pe.value_load(flags[0:1, bass.ds(r, 1)], min_val=0, max_val=1)
                    with pe.If(more):
                        with pe.Fori(0, GROUPS // 2) as i:
                            for buf in range(2):
                                it = r * GROUPS + i * 2 + buf
                                pe.wait_ge(s_awc, it - 1)
                                group(it, buf)
                        pe.wait_ge(s_at, (r + 1) * GROUPS)
                        pe.nop()
                pe.nop()

            pe.wait_ge(s_xwc, NT)
            pe.wait_ge(s_at, GROUPS)
            for o in range(2):
                for c, (a, b) in enumerate(CHUNKS):
                    for s in range(NT):
                        ins = mm(ps[4 + 2 * o + c][:, 0:b - a], xw[:, s, o * 128:(o + 1) * 128], AT[0:NP, s, a:b],
                                 start=(s == 0), stop=(s == NT - 1))
                    ins.then_inc(s_h, 1)
            pe.wait_ge(s_hn, 2)
            for k in range(2):
                if k:
                    pe.wait_ge(s_hn, 3)
                    pe.wait_ge(s_hd, 1)
                for o in range(2):
                    for c, (a, b) in enumerate(CHUNKS):
                        ins = mm(h_bank(1, o, c)[:, 0:b - a], w2g[:, k, o * 128:(o + 1) * 128], nT[:, k, a:b],
                                 start=(k == 0), stop=(k == 1))
                        if k:
                            ins.then_inc(s_h, 1)
            keep_warm(7, WARM[1])
            pe.wait_ge(s_hn, 5)
            for k in range(2):
                if k:
                    pe.wait_ge(s_hn, 6)
                    pe.wait_ge(s_hd, 2)
                for t in range(NT):
                    ins = pe.transpose(back_rows(t)[:, k * 128:(k + 1) * 128], hT[:, k, t:NODES:NT], idt[:, :])
                    if k:
                        ins.then_inc(s_bt, 1)
            keep_warm(2, WARM[2])
            for t in range(NT):
                pe.wait_ge(s_xn, NT + t + 1)
                if t >= 2:
                    pe.wait_ge(s_ntc, NT + t - 1)
                for k in range(2):
                    ins = pe.transpose(ps[t % 2][:, k * NP:(k + 1) * NP], xn[:, t, k * 128:(k + 1) * 128],
                                       idt[0:NP, 0:NP])
                ins.then_inc(s_nt, 1)
                keep_warm(2, 1 if t < NT - 1 else 2)
            pe.wait_ge(s_rt, 48)
            pe.wait_ge(s_ntc, 2 * NT)
            for k in range(2):
                for half in range(2):
                    ins = mm(ps[3][half * EXPERTS:(half + 1) * EXPERTS, 0:(3 - half) * NP], wrs[:, k, :],
                             nT[:, k, 3 * half * NP:(3 + 2 * half) * NP], start=(k == 0), stop=(k == 1))
            ins.then_inc(s_lg, 1)
            pe.wait_ge(s_lgc, 2)
            for n in range(3):
                rows = 2 * EXPERTS if n < 2 else EXPERTS
                ins = pe.transpose(ps[2][0:NP, n * 2 * EXPERTS:n * 2 * EXPERTS + rows], lgT[0:rows, n * NP:(n + 1) * NP],
                                   idt[0:rows, 0:rows])
            ins.then_inc(s_lt, 1)
            pe.wait_ge(s_fb, 32)
            for j in range(4):
                ins = pe.transpose(ps[6][:, j * EXPERTS:(j + 1) * EXPERTS], fb1s[:, j:HID:4], idt[0:EXPERTS, 0:EXPERTS])
            ins.then_inc(s_bi, 1)
            def ranks(bank, wide):
                b = ps[bank]
                ins = mm(b[0:NP, 0:NT * EXPERTS], tri[:, :], Mb[:, :, :].rearrange("p t e -> p (t e)"), start=True, stop=False)
                if wide == NT + 1:
                    mm(b[0:NP, NT * EXPERTS:wide * EXPERTS], ones_b[:, :], Mb[:, NT - 1, :], start=False, stop=False)
                else:
                    mm(b[0:NP, 0:NT * EXPERTS], ones_b[0:1, :], e64b[:, :, :].rearrange("p t e -> p (t e)"),
                       start=False, stop=False)
                for l in range(1, wide):
                    n = min(wide - l, NT - 1)
                    ins = mm(b[0:NP, l * EXPERTS:(l + n) * EXPERTS], ones_b[:, :],
                             Mb[:, 0:n, :].rearrange("p t e -> p (t e)"), start=False, stop=(l == wide - 1))
                return ins

            keep_warm(3, WARM[3])
            pe.wait_ge(s_cst, 5)
            pe.wait_ge(s_m, 1)
            ranks(7, NT + 1).then_inc(s_rk, 1)
            ranks(4, NT).then_inc(s_rk, 1)
            pe.wait_ge(s_gs, 1)
            for t in range(NT):
                ins = pe.transpose(ps[0][0:EXPERTS, t * NP:(t + 1) * NP] if t < 4 else ps[1][0:EXPERTS, 0:NP],
                                   lg[:, t, :], idt[0:NP, 0:NP])
            ins.then_inc(s_gt, 1)
            keep_warm(3, WARM[4])
            for m in range(TOPK * NT):
                pe.wait_ge(s_lh, m + 1)
                ins = mm(ps[5][:, 0:ALL_PAIRS], LO[:, m, :], HI[:, m, :], start=(m == 0), stop=(m == TOPK * NT - 1))
            ins.then_inc(s_ix, 1)

            def rows_T(c, par, slot, gathered):
                pe.wait_ge(s_xg[slot], gathered)
                for k in range(2):
                    ins = pe.transpose(ps[par][:, k * 128:(k + 1) * 128], xg[:, slot, k:D:2], idt[:, :])
                ins.then_inc(s_xt, 1)

            def hidden(par, slot):
                for k in range(2):
                    for half in range(2):
                        rows = slice(half * CAP, (half + 1) * CAP)
                        ins = mm(ps[2 + par][rows, 0:HID], xgT[:, par, k, rows],
                                 w1r(slot)[:, half, k * HID:(k + 1) * HID], start=(k == 0), stop=(k == 1))
                ins.then_inc(s_g1, 1)

            def hidden_T(c, par):
                pe.wait_ge(s_hnc, c + 1)
                for j in range(4):
                    ins = pe.transpose(ps[4 + par][:, j * 128:(j + 1) * 128], hn[:, par, j:HID:4], idt[:, :])
                ins.then_inc(s_hT, 1)

            def result(c, par, slot):
                pe.wait_ge(s_hr, c + 1)
                for j in range(4):
                    for half in range(2):
                        rows = slice(half * CAP, (half + 1) * CAP)
                        ins = mm(ps[6 + par][rows, 0:D], hr[:, par, j, rows],
                                 w2r(slot)[:, half, j * D:(j + 1) * D], start=(j == 0), stop=(j == 3))
                ins.then_inc(s_g2, 1)

            def pair_result(c, m, loads):
                pe.wait_ge(s_w2[m % RING], loads)
                if m >= 2:
                    pe.wait_ge(s_yc, c - 1)
                result(c, m % 2, m % RING)

            def step(i, m):
                c = i * RING + m
                if m >= 2:
                    pe.wait_ge(s_xtc, c - 1)
                rows_T(c, m % 2, m % XG, uses(i, m, XG) * 16)
                if m >= 1:
                    hidden_T(c - 1, (m - 1) % 2)
                pe.wait_ge(s_w1[m % RING], uses(i, m, RING) * 16)
                pe.wait_ge(s_xtc, c + 1)
                hidden(m % 2, m % RING)
                if m >= 1:
                    pair_result(c - 1, m - 1, uses(i, m - 1, RING) * 16)

            keep_warm(3, WARM[5])
            pe.wait_ge(s_gtc, 1)
            pe.wait_ge(s_bic, 1)
            pe.wait_ge(s_ixc, 1)
            for m in range(FIRST):
                step(0, m)
            with pe.Fori(0, (PAIRS - FIRST) // RING) as i:
                for m in range(FIRST, FIRST + RING):
                    step(i, m)
            hidden_T(PAIRS - 1, (PAIRS - 1) % 2)
            pair_result(PAIRS - 1, PAIRS - 1, 16 * uses(0, PAIRS - 1, RING))
            pe.wait_ge(s_yc, PAIRS)
            for t in range(NT):
                ins = mm(gated_bias(t), GT[:, t * NP:(t + 1) * NP], fb2s[:, :], start=True, stop=True)
            ins.then_inc(s_gb, 1)
            pe.wait_ge(s_ovr, 1)
            any_over = pe.value_load(oflag[0:1, 0:1], min_val=0, max_val=1)
            with pe.If(any_over):
                with pe.Fori(0, OVER_PAIRS) as j:
                    used = pe.value_load(oflag[0:1, bass.ds(j, 1)], min_val=0, max_val=1)
                    with pe.If(used):
                        c = j + PAIRS
                        pe.wait_ge(s_yc, c)
                        rows_T(c, 0, over_slot, (j + MAIN_X0 + 1) * 16)
                        pe.wait_ge(s_w1[over_slot], (j * 2 + MAIN_W0 + 2) * 16)
                        pe.wait_ge(s_xtc, c + 1)
                        hidden(0, over_slot)
                        hidden_T(c, 0)
                        pe.wait_ge(s_w2[over_slot], (j * 2 + MAIN_W0 + 2) * 16)
                        result(c, 0, over_slot)
                        pe.nop()
                pe.nop()


_INS = ['x', 'src', 'dst', 'edge_weight', 'L0_gnn_W1', 'L0_gnn_b1', 'L0_gnn_g1', 'L0_gnn_be1', 'L0_gnn_W2',
        'L0_gnn_b2', 'L0_gnn_g2', 'L0_gnn_be2', 'L0_gnn_eps', 'L0_ffn_Wr', 'L0_ffn_br', 'L0_ffn_W1', 'L0_ffn_b1',
        'L0_ffn_W2', 'L0_ffn_b2']


def kernel(**inputs):
    import numpy as np
    import concourse.bacc as bacc
    from concourse import mybir
    from concourse.bass_utils import run_bass_kernel_spmd

    nc = bacc.Bacc("TRN2", target_bir_lowering=False, num_devices=1)
    arrays, args = {}, []
    for name in _INS:
        a = np.ascontiguousarray(inputs[name])
        arrays[f"in_{name}"] = a
        args.append(nc.dram_tensor(f"in_{name}", a.shape, mybir.dt.from_np(a.dtype), kind="ExternalInput").ap())
    args.append(nc.dram_tensor("out_0", (NODES, D), mybir.dt.float32, kind="ExternalOutput").ap())
    gnn_moe(nc, *args)
    r = run_bass_kernel_spmd(nc, [arrays], core_ids=[0])
    return r.results[0]["out_0"]
```
